# Optimizing a Trainium2 kernel written in Bass

```python
import numpy as np
import jax
import jax.numpy as jnp

def _softmax(x, axis=-1):
    return jax.nn.softmax(x, axis=axis)

def _gelu(x):
    return jax.nn.gelu(x, approximate=True)

def _silu(x):
    return jax.nn.silu(x)

def _sigmoid(x):
    return jax.nn.sigmoid(x)

def _layernorm(x, axis=-1, eps=1e-05):
    m = jnp.mean(x, axis=axis, keepdims=True)
    v = jnp.var(x, axis=axis, keepdims=True)
    return (x - m) / jnp.sqrt(v + eps)

def _scatter_add(tgt, idx, src, axis=0):
    return tgt.at[idx].add(src)

def _segment_sum(src, seg, n):
    return jax.ops.segment_sum(src, seg, n)
kernel_name = 'mk_adj_ffn_d1_adj_r2_4b586a'

def setup_inputs(seed: int=0):
    np.random.seed(seed)
    _w = jnp.asarray

    def _rec_inputs():
        import jax
        import jax.numpy as jnp
        _gk = jax.random.key(seed)
        x = -0.001547 + 1.001 * jax.random.normal(jax.random.fold_in(_gk, 1), (64, 128, 128), jnp.float32)
        _a = jax.random.bernoulli(jax.random.fold_in(_gk, 2), 0.015625, (64, 128, 128))
        _a = jnp.logical_or(_a, jnp.swapaxes(_a, -1, -2))
        _a = jnp.logical_or(_a, jnp.eye(128, dtype=bool))
        adj = _a.astype(jnp.int32)
        _nm = jnp.ones((64, 128), dtype=bool)
        nodemask = jnp.where(_nm, 1.0, 0.0).astype(jnp.float32)
        return (x, adj, nodemask)
    x, adj, nodemask = _rec_inputs()

    def _L0_gnn_setup():
        import jax, jax.numpy as jnp
        import numpy as np
        D_MODEL = 128
        NUM_REL = 40

        def _direction(x, W, Wg, b, bg, adj, rel_ids):
            h = x @ W.T
            g = h @ Wg.T
            vals = (h[:, :, None, :] + b) * jax.nn.sigmoid(g[:, :, None, :] + bg)
            onehot = (adj[..., None] == rel_ids).astype(h.dtype)
            return jnp.einsum('bnmr,bmrd->bnd', onehot, vals)
        key = jax.random.key(seed)
        ks = jax.random.split(key, 16)
        B, N, d = (2, 256, D_MODEL)
        s = 0.02
        inp = {'node': jax.random.normal(ks[0], (B, N, d), dtype=jnp.float32), 'node_mask': jnp.ones((B, N), dtype=jnp.float32), 'adj_mat': jax.random.randint(ks[1], (B, N, N), 0, 41, dtype=jnp.int32), 'W_fwd': jax.random.normal(ks[2], (d, d), dtype=jnp.float32) * s, 'W_bwd': jax.random.normal(ks[3], (d, d), dtype=jnp.float32) * s, 'W_loop': jax.random.normal(ks[4], (d, d), dtype=jnp.float32) * s, 'Wg_fwd': jax.random.normal(ks[5], (d, d), dtype=jnp.float32) * s, 'Wg_bwd': jax.random.normal(ks[6], (d, d), dtype=jnp.float32) * s, 'Wg_loop': jax.random.normal(ks[7], (d, d), dtype=jnp.float32) * s, 'b_fwd': jax.random.normal(ks[8], (NUM_REL - 1, d), dtype=jnp.float32) * s, 'b_bwd': jax.random.normal(ks[9], (NUM_REL - 1, d), dtype=jnp.float32) * s, 'b_loop': jax.random.normal(ks[10], (1, d), dtype=jnp.float32) * s, 'bg_fwd': jax.random.normal(ks[11], (NUM_REL - 1, d), dtype=jnp.float32) * s, 'bg_bwd': jax.random.normal(ks[12], (NUM_REL - 1, d), dtype=jnp.float32) * s, 'bg_loop': jax.random.normal(ks[13], (1, d), dtype=jnp.float32) * s}
        return inp
    _L0_gnn_all = _L0_gnn_setup()
    _L0_gnn_in = {k: v for k, v in _L0_gnn_all.items() if k in ('W_fwd', 'W_bwd', 'W_loop', 'Wg_fwd', 'Wg_bwd', 'Wg_loop', 'b_fwd', 'b_bwd', 'b_loop', 'bg_fwd', 'bg_bwd', 'bg_loop')}
    del _L0_gnn_all

    def _L0_ffn_setup():
        import jax, jax.numpy as jnp
        import numpy as np
        E, D, H, TOP_K = (6, 128, 128, 2)
        ROUTER_H = D // 2
        key = jax.random.key(seed)
        ks = jax.random.split(key, 12)
        s = 1.0 / np.sqrt(D)
        sh = 1.0 / np.sqrt(H)
        sr = 1.0 / np.sqrt(ROUTER_H)
        return {'features': jax.random.normal(ks[0], (8, 2048, D), dtype=jnp.float32), 'router_w1': jax.random.uniform(ks[1], (D, ROUTER_H), jnp.float32, -s, s), 'router_b1': jnp.zeros((ROUTER_H,), jnp.float32), 'router_w2': jax.random.uniform(ks[2], (ROUTER_H, E), jnp.float32, -sr, sr), 'router_b2': jnp.zeros((E,), jnp.float32), 'expert_w1': jax.random.uniform(ks[3], (E, D, H), jnp.float32, -s, s), 'expert_b1': jnp.zeros((E, H), jnp.float32), 'expert_w2': jax.random.uniform(ks[4], (E, H, H), jnp.float32, -sh, sh), 'expert_b2': jnp.zeros((E, H), jnp.float32), 'expert_w3': jax.random.uniform(ks[5], (E, H, D), jnp.float32, -sh, sh), 'expert_b3': jnp.zeros((E, D), jnp.float32)}
    _L0_ffn_all = _L0_ffn_setup()
    _L0_ffn_in = {k: v for k, v in _L0_ffn_all.items() if k in ('router_w1', 'router_b1', 'router_w2', 'router_b2', 'expert_w1', 'expert_b1', 'expert_w2', 'expert_b2', 'expert_w3', 'expert_b3')}
    del _L0_ffn_all
    return {'x': x, 'adj': adj, 'nodemask': nodemask, 'L0_gnn_W_fwd': _L0_gnn_in['W_fwd'], 'L0_gnn_W_bwd': _L0_gnn_in['W_bwd'], 'L0_gnn_W_loop': _L0_gnn_in['W_loop'], 'L0_gnn_Wg_fwd': _L0_gnn_in['Wg_fwd'], 'L0_gnn_Wg_bwd': _L0_gnn_in['Wg_bwd'], 'L0_gnn_Wg_loop': _L0_gnn_in['Wg_loop'], 'L0_gnn_b_fwd': _L0_gnn_in['b_fwd'], 'L0_gnn_b_bwd': _L0_gnn_in['b_bwd'], 'L0_gnn_b_loop': _L0_gnn_in['b_loop'], 'L0_gnn_bg_fwd': _L0_gnn_in['bg_fwd'], 'L0_gnn_bg_bwd': _L0_gnn_in['bg_bwd'], 'L0_gnn_bg_loop': _L0_gnn_in['bg_loop'], 'L0_ffn_router_w1': _L0_ffn_in['router_w1'], 'L0_ffn_router_b1': _L0_ffn_in['router_b1'], 'L0_ffn_router_w2': _L0_ffn_in['router_w2'], 'L0_ffn_router_b2': _L0_ffn_in['router_b2'], 'L0_ffn_expert_w1': _L0_ffn_in['expert_w1'], 'L0_ffn_expert_b1': _L0_ffn_in['expert_b1'], 'L0_ffn_expert_w2': _L0_ffn_in['expert_w2'], 'L0_ffn_expert_b2': _L0_ffn_in['expert_b2'], 'L0_ffn_expert_w3': _L0_ffn_in['expert_w3'], 'L0_ffn_expert_b3': _L0_ffn_in['expert_b3']}

def reference(x, adj, nodemask, L0_gnn_W_fwd, L0_gnn_W_bwd, L0_gnn_W_loop, L0_gnn_Wg_fwd, L0_gnn_Wg_bwd, L0_gnn_Wg_loop, L0_gnn_b_fwd, L0_gnn_b_bwd, L0_gnn_b_loop, L0_gnn_bg_fwd, L0_gnn_bg_bwd, L0_gnn_bg_loop, L0_ffn_router_w1, L0_ffn_router_b1, L0_ffn_router_w2, L0_ffn_router_b2, L0_ffn_expert_w1, L0_ffn_expert_b1, L0_ffn_expert_w2, L0_ffn_expert_b2, L0_ffn_expert_w3, L0_ffn_expert_b3):
    import jax
    import jax.numpy as jnp

    def _L0_gnn_ref(node, node_mask, adj_mat, W_fwd, W_bwd, W_loop, Wg_fwd, Wg_bwd, Wg_loop, b_fwd, b_bwd, b_loop, bg_fwd, bg_bwd, bg_loop):
        import jax, jax.numpy as jnp
        import numpy as np
        D_MODEL = 128
        NUM_REL = 40

        def _direction(x, W, Wg, b, bg, adj, rel_ids):
            h = x @ W.T
            g = h @ Wg.T
            vals = (h[:, :, None, :] + b) * jax.nn.sigmoid(g[:, :, None, :] + bg)
            onehot = (adj[..., None] == rel_ids).astype(h.dtype)
            return jnp.einsum('bnmr,bmrd->bnd', onehot, vals)
        rels = jnp.arange(2, NUM_REL + 1, dtype=adj_mat.dtype)
        rel1 = jnp.array([1], dtype=adj_mat.dtype)
        adj_t = jnp.swapaxes(adj_mat, -1, -2)
        out = _direction(node, W_fwd, Wg_fwd, b_fwd, bg_fwd, adj_mat, rels)
        out = out + _direction(node, W_bwd, Wg_bwd, b_bwd, bg_bwd, adj_t, rels)
        out = out + _direction(node, W_loop, Wg_loop, b_loop, bg_loop, adj_t, rel1)
        return jax.nn.relu(out)

    def _L0_ffn_ref(features, router_w1, router_b1, router_w2, router_b2, expert_w1, expert_b1, expert_w2, expert_b2, expert_w3, expert_b3):
        import jax, jax.numpy as jnp
        import numpy as np
        E, D, H, TOP_K = (6, 128, 128, 2)
        ROUTER_H = D // 2
        rh = jax.nn.relu(features @ router_w1 + router_b1)
        expert_logits = jax.nn.softmax(rh @ router_w2 + router_b2, axis=-1)
        top_w, top_i = jax.lax.top_k(expert_logits, TOP_K)
        routing_weights = jax.nn.softmax(top_w, axis=-1)
        h1 = jax.nn.relu(jnp.einsum('bsd,edh->bseh', features, expert_w1) + expert_b1)
        h2 = jax.nn.relu(jnp.einsum('bseh,ehf->bsef', h1, expert_w2) + expert_b2)
        expert_out = jnp.einsum('bsef,efo->bseo', h2, expert_w3) + expert_b3
        sel = jnp.take_along_axis(expert_out, top_i[:, :, :, None], axis=2)
        combined = jnp.sum(sel * routing_weights[..., None], axis=2)
        return combined
    x = x + _L0_gnn_ref(_layernorm(x, axis=-1), nodemask, adj, L0_gnn_W_fwd, L0_gnn_W_bwd, L0_gnn_W_loop, L0_gnn_Wg_fwd, L0_gnn_Wg_bwd, L0_gnn_Wg_loop, L0_gnn_b_fwd, L0_gnn_b_bwd, L0_gnn_b_loop, L0_gnn_bg_fwd, L0_gnn_bg_bwd, L0_gnn_bg_loop)
    x = x + _L0_ffn_ref(_layernorm(x, axis=-1), L0_ffn_router_w1, L0_ffn_router_b1, L0_ffn_router_w2, L0_ffn_router_b2, L0_ffn_expert_w1, L0_ffn_expert_b1, L0_ffn_expert_w2, L0_ffn_expert_b2, L0_ffn_expert_w3, L0_ffn_expert_b3)
    return x

_drawn_inputs = setup_inputs


def setup_inputs(seed=0):
    import zlib

    import numpy as np

    out = dict(_drawn_inputs(seed))
    spreads = {'L0_ffn_router_b1': (0.0, 0.1),
     'L0_ffn_router_b2': (0.0, 0.1),
     'L0_ffn_expert_b1': (0.0, 0.729),
     'L0_ffn_expert_b2': (0.0, 0.272),
     'L0_ffn_expert_b3': (0.0, 0.1)}
    factors = {'L0_gnn_Wg_loop': 7.093, 'L0_gnn_bg_loop': 22.013}
    for name, (base, spread) in spreads.items():
        noise = np.random.default_rng([zlib.crc32(name.encode()), seed]).standard_normal(out[name].shape)
        drawn = base * np.exp(spread * noise) if base else spread * noise
        out[name] = jnp.asarray(drawn.astype(out[name].dtype))
    for name, factor in factors.items():
        out[name] = (out[name] * factor).astype(out[name].dtype)
    return out
```

```python
from contextlib import ExitStack

import concourse.bass as bass
from concourse import mybir

F32 = mybir.dt.float32
F32R = mybir.dt.float32r
I32 = mybir.dt.int32
ALU = mybir.AluOpType
ACT = mybir.ActivationFunctionType
AX = mybir.AxisListType

P = 128
GRAPHS = 64
GB = 4
TOK = GB * P
GROUPS = GRAPHS // GB
EXPERTS = 6
STEPS = EXPERTS
ROUTER_H = 64
RELS = 39
REL_CHUNK = 13
L2_LAG = 3
L3_LAG = 5
R1_RING = 6
R2_RING = 3
LN_EPS = 1e-5
BLK = 32
DMA = 16


def wait(eng, sem, value):
    if not (isinstance(value, int) and value <= 0):
        eng.wait_ge(sem, value)


def wait_apart(eng, sem, value, reached):
    if not isinstance(value, int):
        value = eng.snap(eng.to_reg(value))
    eng.wait_ge(reached, 1)
    wait(eng, sem, value)


def live(g):
    return not isinstance(g, int) or 0 <= g < GROUPS


def pipeline(eng, iteration, run=0, ahead=2):
    last = (GROUPS - ahead) // 2
    for i in range(-2, 2):
        iteration(i, i + GROUPS * run, i % 2)
    with eng.Fori(1, last) as pair:
        for parity in range(2):
            i = pair * 2 + parity
            iteration(i, i + GROUPS * run, parity)
    for i in range(2 * last, GROUPS + 2):
        iteration(i, i + GROUPS * run, i % 2)


def adj_ffn_kernel(nc, x, adj, w_fwd, w_bwd, w_loop, wg_fwd, wg_bwd, wg_loop, b_fwd, b_bwd, b_loop,
                   bg_fwd, bg_bwd, bg_loop, router_w1, router_b1, router_w2, router_b2,
                   expert_w1, expert_b1, expert_w2, expert_b2, expert_w3, expert_b3, out):
    with ExitStack() as ctx:
        ctx.enter_context(nc.allow_non_contiguous_dma(reason="bias columns and rows of tokens"))

        def sb(name, shape, dt=F32):
            return ctx.enter_context(nc.sbuf_tensor(name, shape, dt))

        def sem(name):
            return ctx.enter_context(nc.semaphore(name))

        ident = sb("ident", [P, P])
        raw_w = [sb(f"raw_w{n}", [P, EXPERTS, P]) for n in range(3)]
        w_hi = [sb(f"w_hi{n}", [P, EXPERTS, P], F32R) for n in range(3)]
        w_lo = [sb(f"w_lo{n}", [P, EXPERTS, P], F32R) for n in range(3)]
        bias1 = sb("bias1", [P, EXPERTS])
        bias2 = sb("bias2", [P, EXPERTS])
        raw_b3 = sb("raw_b3", [P, P])
        b3_split = sb("b3_split", [P, P], F32R)
        select = sb("select", [P, EXPERTS, P], F32R)
        raw_router = sb("raw_router", [P, P])
        router_hi = sb("router_hi", [P, P], F32R)
        router_lo = sb("router_lo", [P, P], F32R)
        router_bias = sb("router_bias", [P, 1])
        logit_w = sb("logit_w", [P, EXPERTS])
        logit_bias = sb("logit_bias", [P, GB, EXPERTS])
        priority = sb("priority", [P, GB, EXPERTS])
        minus_half = sb("minus_half", [P, GB])
        raw_loop = sb("raw_loop", [P, 2, P])
        wg_t = sb("wg_t", [P, P])
        hg = sb("hg", [P, 2, P])
        hg_hi = sb("hg_hi", [P, 2, P], F32R)
        hg_lo = sb("hg_lo", [P, 2, P], F32R)
        raw_hg_bias = sb("raw_hg_bias", [P, 2, 2, P])
        hg_bias = sb("hg_bias", [P, 2, 2, P], F32R)
        ones = sb("ones", [P, P], F32R)

        X = sb("X", [P, GROUPS * TOK])
        adj_in = sb("adj_in", [P, 2, TOK], I32)
        loop_edges = sb("loop_edges", [P, TOK], F32R)
        over_one = sb("over_one", [P, TOK])
        over_sum = sb("over_sum", [P, 2])
        over_all = sb("over_all", [P, 1])
        minus_one = sb("minus_one", [P, 1])
        stats = sb("stats", [P, 2, GB, 6])
        mean_var = sb("mean_var", [P, 2, GB, 2])
        var_eps = sb("var_eps", [P, 2, GB])
        rstd = sb("rstd", [P, 2, GB])
        xn = sb("xn", [P, 2, TOK])
        xg_hi = sb("xg_hi", [P, TOK], F32R)
        xg_lo = sb("xg_lo", [P, TOK], F32R)
        gate = sb("gate", [P, GB, P])
        vals = sb("vals", [P, GB, P])
        vals_hi = sb("vals_hi", [P, TOK], F32R)
        vals_lo = sb("vals_lo", [P, TOK], F32R)
        xf_hi = sb("xf_hi", [P, 2, TOK], F32R)
        xf_lo = sb("xf_lo", [P, 2, TOK], F32R)
        router_h = sb("router_h", [P, TOK])
        rt = {n: sb("rt_" + n, [P, GB, EXPERTS]) for n in
              ("z", "shifted", "exp", "p", "rest", "hit", "rank", "first", "second", "both", "diff", "tilt", "w")}
        rc = {n: sb("rc_" + n, [P, GB]) for n in
              ("max", "sum", "rsum", "p1", "p2", "best1", "best2", "gap", "tanh")}
        w_parts = sb("w_parts", [P, GB, P])
        w_blocks_f = w_parts[:, :, :].rearrange("p b (q c) -> p b q c", c=BLK)
        w_blocks = w_parts[:, :, :].bitcast(F32R).rearrange("p b (q c) -> p b q c", c=BLK)
        w_rows = sb("w_rows", [P, TOK], F32R)
        u1 = sb("u1", [P, 2, TOK])
        r1_hi = sb("r1_hi", [P, R1_RING, TOK], F32R)
        r1_lo = sb("r1_lo", [P, R1_RING, TOK], F32R)
        u2 = sb("u2", [P, 2, TOK])
        v2 = sb("v2", [P, 2, TOK])
        r2_hi = sb("r2_hi", [P, R2_RING, TOK], F32R)
        r2_lo = sb("r2_lo", [P, R2_RING, TOK], F32R)
        ffn_t = sb("ffn_t", [P, TOK])

        flag = sb("flag", [1, 1], I32)
        gen_x = sb("gen_x", [P, P])
        gen_adj = sb("gen_adj", [P, P], I32)
        gen_xn = sb("gen_xn", [P, P])
        gen_xn_t = sb("gen_xn_t", [P, P])
        gen_rel = sb("gen_rel", [P, P])
        gen_rel_t = sb("gen_rel_t", [P, P])
        gen_hg = sb("gen_hg", [P, 2, P])
        gen_w = sb("gen_w", [P, 2, P])
        gen_bias = sb("gen_bias", [P, 2, REL_CHUNK, P])
        gen_vals = sb("gen_vals", [P, REL_CHUNK, P])
        gen_gate = sb("gen_gate", [P, REL_CHUNK, P])
        gen_hot = sb("gen_hot", [P, REL_CHUNK, P])
        gen_number = sb("gen_number", [P, RELS + 1])

        ps_l1 = [ctx.enter_context(nc.psum_tensor(f"ps_l1_{n}", [P, TOK], F32)) for n in range(2)]
        ps_l2 = [ctx.enter_context(nc.psum_tensor(f"ps_l2_{n}", [P, TOK], F32)) for n in range(2)]
        ps_l3 = ctx.enter_context(nc.psum_tensor("ps_l3", [P, TOK], F32))
        ps_w = ctx.enter_context(nc.psum_tensor("ps_w", [P, TOK], F32))
        ps_side = ctx.enter_context(nc.psum_tensor("ps_side", [P, 2 * TOK], F32))
        ps_a, ps_b = ps_side[:, 0:TOK], ps_side[:, TOK:2 * TOK]
        ps_hg = ps_side[:, :].rearrange("p (b c) -> p b c", c=2 * P)

        s_w_loaded = sem("s_w_loaded")
        s_small_loaded = sem("s_small_loaded")
        s_zeroed = sem("s_zeroed")
        s_ident = sem("s_ident")
        s_loop_t = sem("s_loop_t")
        s_gate_w = sem("s_gate_w")
        s_prep = sem("s_prep")
        s_const = sem("s_const")
        s_x_loaded = [sem(f"s_x_loaded{n}") for n in range(2)]
        s_adj_loaded = [sem(f"s_adj_loaded{n}") for n in range(2)]
        s_stored = sem("s_stored")
        s_stats = [sem(f"s_stats{n}") for n in range(2)]
        s_mean_var = [sem(f"s_mean_var{n}") for n in range(2)]
        s_ln1 = sem("s_ln1")
        s_rstd1 = sem("s_rstd1")
        s_xn1 = sem("s_xn1")
        s_t1 = sem("s_t1")
        s_xg_hi = sem("s_xg_hi")
        s_xg_lo = sem("s_xg_lo")
        s_hg = sem("s_hg")
        s_gate = sem("s_gate")
        s_vals = sem("s_vals")
        s_vals_hi = sem("s_vals_hi")
        s_vals_lo = sem("s_vals_lo")
        s_edges = sem("s_edges")
        s_over = sem("s_over")
        s_over_all = sem("s_over_all")
        s_agg = sem("s_agg")
        s_x1 = sem("s_x1")
        s_ln2 = sem("s_ln2")
        s_rstd2 = sem("s_rstd2")
        s_xn2 = sem("s_xn2")
        s_t2 = sem("s_t2")
        s_xf_hi = sem("s_xf_hi")
        s_xf_lo = sem("s_xf_lo")
        s_rh = sem("s_rh")
        s_router_h = sem("s_router_h")
        s_logits = sem("s_logits")
        s_route = sem("s_route")
        s_route_act = sem("s_route_act")
        s_w_t = sem("s_w_t")
        s_w_rows = sem("s_w_rows")
        s_l1 = sem("s_l1")
        s_r1_hi = sem("s_r1_hi")
        s_u1 = sem("s_u1")
        s_r1_lo = sem("s_r1_lo")
        s_l2 = sem("s_l2")
        s_wb = sem("s_wb")
        s_u2 = sem("s_u2")
        s_v2 = sem("s_v2")
        s_r2_hi = sem("s_r2_hi")
        s_r2_lo = sem("s_r2_lo")
        s_l3 = sem("s_l3")
        s_ffn_t = sem("s_ffn_t")
        s_out_t = sem("s_out_t")
        s_final = sem("s_final")
        s_over_sum = sem("s_over_sum")
        s_flag = sem("s_flag")
        s_gen_w_loaded = sem("s_gen_w_loaded")
        s_gen_w_t = sem("s_gen_w_t")
        s_gen_w = sem("s_gen_w")
        s_gen_gate_w = sem("s_gen_gate_w")
        s_gen_bias = sem("s_gen_bias")
        s_gen_const = sem("s_gen_const")
        s_gen_loaded = sem("s_gen_loaded")
        s_gen_stats = sem("s_gen_stats")
        s_gen_mean = sem("s_gen_mean")
        s_gen_var = sem("s_gen_var")
        s_gen_rstd = sem("s_gen_rstd")
        s_gen_in = sem("s_gen_in")
        s_gen_t = sem("s_gen_t")
        s_gen_t_copied = sem("s_gen_t_copied")
        s_gen_hg = sem("s_gen_hg")
        s_gen_step = sem("s_gen_step")
        s_gen_gate = sem("s_gen_gate")
        s_gen_sum = sem("s_gen_sum")
        s_gen_acc = sem("s_gen_acc")
        s_gen_x_loaded = sem("s_gen_x_loaded")
        s_gen_x1 = sem("s_gen_x1")
        GEN_STEPS = 5
        ROUTE = 24

        x_v = x.rearrange("(g b) p d -> p g b d", b=GB)
        adj_v = adj.rearrange("(g b) p n -> p g b n", b=GB)
        out_v = out.rearrange("(g b) p d -> p g b d", b=GB)

        def X_of(g, b=None):
            if b is None:
                return X[:, bass.ds(g * TOK, TOK)]
            return X[:, bass.ds(g * TOK + b * P, P)]

        def tok3(ap):
            return ap.rearrange("p (b d) -> p b d", b=GB)

        N_BIG, N_SMALL = 9, 19
        N_PREP = 19
        N_CONST = 3 + EXPERTS + 2

        def loads(g):
            return DMA * (g // 2 + 1)


        def load_inputs(sp):
            sp.dma_start(raw_loop[:, 0], w_loop).then_inc(s_small_loaded, DMA)
            sp.dma_start(raw_loop[:, 1], wg_loop).then_inc(s_small_loaded, DMA)
            sp.wait_ge(s_zeroed, 3)
            for row in (0, BLK):
                for twice in range(2):
                    sp.dma_start(raw_hg_bias[row:row + 1, twice, 0], b_loop).then_inc(s_small_loaded, DMA)
                    sp.dma_start(raw_hg_bias[row:row + 1, twice, 1], bg_loop).then_inc(s_small_loaded, DMA)
            for half in range(2):
                sp.dma_start(raw_router[:, half * ROUTER_H:(half + 1) * ROUTER_H], router_w1)\
                    .then_inc(s_small_loaded, DMA)
                sp.dma_start(router_bias[half * ROUTER_H:(half + 1) * ROUTER_H],
                             router_b1.rearrange("(h a) -> h a", a=1)).then_inc(s_small_loaded, DMA)
            sp.dma_start(logit_w[0:ROUTER_H], router_w2).then_inc(s_small_loaded, DMA)
            for b in range(GB):
                sp.dma_start(logit_bias[:, b], router_b2.partition_broadcast(P)).then_inc(s_small_loaded, DMA)
            for n, w in enumerate((expert_w1, expert_w2, expert_w3)):
                sp.dma_start(raw_w[n][:, :, :], w.rearrange("e d f -> d e f")).then_inc(s_w_loaded, DMA)
            sp.dma_start(bias1[:, :], expert_b1.rearrange("e h -> h e")).then_inc(s_w_loaded, DMA)
            sp.dma_start(bias2[:, :], expert_b2.rearrange("e h -> h e")).then_inc(s_w_loaded, DMA)
            for n in range(4):
                sp.dma_start(raw_b3[n * BLK:n * BLK + EXPERTS], expert_b3).then_inc(s_w_loaded, DMA)

        def sp_pipeline(sp, run):
            def load(g, parity):
                wait_apart(sp, s_ln1, g - 1, s_zeroed)
                wait(sp, s_edges, g - 1)
                wait(sp, s_over, g - 1)
                sp.dma_start(tok3(X_of(g)), x_v[:, bass.ds(g, 1)].rearrange("p g b d -> p (g b) d"))\
                    .then_inc(s_x_loaded[parity], DMA)
                sp.dma_start(tok3(adj_in[:, parity]), adj_v[:, bass.ds(g, 1)].rearrange("p g b d -> p (g b) d"))\
                    .then_inc(s_adj_loaded[parity], DMA)

            def iteration(i, n, parity):
                if run == 0 and live(i + 3):
                    load(i + 3, 1 - parity)
                if live(i - 2):
                    wait_apart(sp, s_final, n - 1, s_zeroed)
                    sp.dma_start(out_v[:, bass.ds(i - 2, 1)].rearrange("p g b d -> p (g b) d"), tok3(X_of(i - 2)))\
                        .then_inc(s_stored, DMA)

            if run == 0:
                load(0, 0)
                load_inputs(sp)
            pipeline(sp, iteration, run, ahead=4)
            sp.wait_ge(s_stored, DMA * GROUPS * (run + 1))

        def pool_constants(pool):
            nc.gpsimd.memset(ident[:, :], 0.0).then_inc(s_ident, 1)
            nc.gpsimd.memset(raw_hg_bias[:, :, :, :], 0.0).then_inc(s_zeroed, 1)
            nc.gpsimd.memset(logit_w[:, :], 0.0).then_inc(s_zeroed, 1)
            nc.gpsimd.memset(raw_b3[:, :], 0.0).then_inc(s_zeroed, 1)
            pool.wait_ge(s_ident, 1)
            nc.gpsimd.affine_select(out=ident[:, :], in_=ident[:, :], compare_op=ALU.not_equal, fill=1.0,
                                    base=0, pattern=[[-1, P]], channel_multiplier=1).then_inc(s_ident, 1)
            nc.gpsimd.memset(minus_half[:, :], -0.5).then_inc(s_const, 1)
            nc.gpsimd.memset(ones[:, :].bitcast(F32), 1.0).then_inc(s_const, 1)
            nc.gpsimd.memset(w_parts[:, :, :], 0.0).then_inc(s_const, 1)
            for e in range(EXPERTS):
                nc.gpsimd.memset(priority[:, :, e:e + 1], float(EXPERTS - e)).then_inc(s_const, 1)
            nc.gpsimd.memset(minus_one[:, :], -1.0).then_inc(s_const, 1)
            nc.gpsimd.memset(over_all[:, :], 0.0).then_inc(s_const, 1)
            pool.wait_ge(s_const, 1)

        def pool_pipeline(pool, run):
            def rstd_of(norm, c, s_stats, s_rstd, s_xn):
                pool.wait_ge(s_stats, c + 1)
                wait(pool, s_xn, c)
                nc.gpsimd.tensor_tensor(rstd[:, norm], var_eps[:, norm], minus_half[:, :], ALU.pow)\
                    .then_inc(s_rstd, 1)

            def iteration(i, n, parity):
                for s in range(STEPS):
                    if s == 4 and run == 0 and live(i + 2):
                        rstd_of(0, n + 2, s_ln1, s_rstd1, s_xn1)
                    if live(i if s >= L2_LAG else i - 1):
                        k = EXPERTS * n + s - L2_LAG
                        r = s % R2_RING
                        pool.wait_ge(s_r2_hi, k + 1)
                        wait(pool, s_l3, k + 1 - R2_RING)
                        nc.gpsimd.tensor_tensor(r2_lo[:, r], v2[:, s % 2], r2_hi[:, r].bitcast(F32), ALU.subtract)\
                            .then_inc(s_r2_lo, 1)
                    if s == 3 and live(i + 1):
                        rstd_of(1, n + 1, s_ln2, s_rstd2, s_xn2)
                    if live(i):
                        k = EXPERTS * n + s
                        pool.wait_ge(s_u1, k + 1)
                        wait(pool, s_l2, k + 1 - R1_RING)
                        nc.gpsimd.tensor_tensor(r1_lo[:, s], u1[:, s % 2], r1_hi[:, s].bitcast(F32), ALU.subtract)\
                            .then_inc(s_r1_lo, 1)

            pipeline(pool, iteration, run)

        def act_pipeline(act, run):
            gnn = run == 0

            def iteration(i, n, parity):
                for s in range(STEPS):
                    if s == 0 and live(i):
                        act.wait_ge(s_rh, n + 1)
                        wait(act, s_logits, n)
                        nc.scalar.activation(router_h[:, :], ps_b, ACT.Relu, bias=router_bias[:, :])\
                            .then_inc(s_router_h, 1)
                    if s == 0 and gnn and live(i + 1):
                        act.wait_ge(s_t1, n + 2)
                        wait(act, s_hg, n + 1)
                        nc.scalar.activation(xg_hi[:, :], ps_a, ACT.Copy).then_inc(s_xg_hi, 1)
                    if s == 1 and gnn and live(i + 1):
                        act.wait_ge(s_hg, n + 2)
                        wait(act, s_vals, n + 1)
                        nc.scalar.activation(gate[:, :, :], ps_hg[:, :, P:2 * P], ACT.Tanh, scale=0.5)\
                            .then_inc(s_gate, 1)
                    if s == 2 and live(i):
                        act.wait_ge(s_route, ROUTE * n + 18)
                        nc.scalar.activation(rc["tanh"][:, :], rc["gap"][:, :], ACT.Tanh, scale=0.5)\
                            .then_inc(s_route_act, 1)
                    if s == 3 and live(i):
                        act.wait_ge(s_w_t, n + 1)
                        nc.scalar.activation(w_rows[:, :], ps_w[:, :], ACT.Copy).then_inc(s_w_rows, 1)
                    if s == 5 and live(i + 1):
                        act.wait_ge(s_t2, n + 2)
                        wait(act, s_l1, EXPERTS * n)
                        nc.scalar.activation(xf_hi[:, 1 - parity], ps_a, ACT.Copy).then_inc(s_xf_hi, 1)
                    if s == 5 and live(i - 1):
                        act.wait_ge(s_l3, EXPERTS * n)
                        wait(act, s_out_t, n - 1)
                        nc.scalar.activation(ffn_t[:, :], ps_l3[:, :], ACT.Copy).then_inc(s_ffn_t, 1)
                    if live(i if s >= L2_LAG else i - 1):
                        e = (s - L2_LAG) % EXPERTS
                        k = EXPERTS * n + s - L2_LAG
                        act.wait_ge(s_l2, k + 1)
                        wait(act, s_v2, k - 1)
                        nc.scalar.activation(u2[:, s % 2], ps_l2[s % 2][:, :], ACT.Relu, bias=bias2[:, e:e + 1])\
                            .then_inc(s_u2, 1)
                    if s == 1 and live(i):
                        act.wait_ge(s_route, ROUTE * n + 3)
                        nc.scalar.activation(rt["exp"][:, :, :], rt["shifted"][:, :, :], ACT.Exp)\
                            .then_inc(s_route_act, 1)
                    if live(i):
                        k = EXPERTS * n + s
                        act.wait_ge(s_l1, k + 1)
                        wait(act, s_l2, k + 1 - R1_RING)
                        nc.scalar.activation(r1_hi[:, s], ps_l1[s % 2][:, :], ACT.Relu, bias=bias1[:, s:s + 1])\
                            .then_inc(s_r1_hi, 1)
                        wait(act, s_r1_lo, k - 1)
                        nc.scalar.activation(u1[:, s % 2], ps_l1[s % 2][:, :], ACT.Relu, bias=bias1[:, s:s + 1])\
                            .then_inc(s_u1, 1)
                    if s == 1 and gnn and live(i + 1):
                        act.wait_ge(s_vals, n + 2)
                        wait(act, s_agg, n + 1)
                        nc.scalar.activation(tok3(vals_hi[:, :]), vals[:, :, :], ACT.Copy).then_inc(s_vals_hi, 1)
                    if s == 3 and gnn and live(i + 2):
                        act.wait_ge(s_adj_loaded[parity], loads(i + 2))
                        wait(act, s_over, n + 2)
                        wait(act, s_over_all, n + 1)
                        nc.scalar.activation(over_one[:, :], adj_in[:, parity], ACT.Relu, bias=minus_one[:, :],
                                             accum_out=over_sum[:, parity:parity + 1]).then_inc(s_over, 1)

            if run == 0:
                act.wait_ge(s_w_loaded, DMA * N_BIG)
                act.wait_ge(s_small_loaded, DMA * N_SMALL)
                act.wait_ge(s_const, 3 + EXPERTS + 1)
            pipeline(act, iteration, run)

        def dve_setup(dve):
            v = nc.vector
            dve.wait_ge(s_small_loaded, DMA * N_SMALL)
            dve.wait_ge(s_zeroed, 3)
            v.tensor_scalar(raw_hg_bias[:, :, 0], raw_hg_bias[:, :, 0], 0.5, None, ALU.mult).then_inc(s_prep, 1)
            dve.wait_ge(s_prep, 1)
            v.tensor_copy(hg_bias[:, :, :, :], raw_hg_bias[:, :, :, :]).then_inc(s_prep, 1)
            dve.wait_ge(s_prep, 2)
            v.tensor_tensor(hg_bias[BLK:2 * BLK], raw_hg_bias[BLK:2 * BLK], hg_bias[BLK:2 * BLK].bitcast(F32),
                            ALU.subtract).then_inc(s_prep, 1)
            dve.wait_ge(s_loop_t, 2)
            v.tensor_scalar(hg[:, 0], ps_l1[0][:, 0:P], 0.5, None, ALU.mult).then_inc(s_prep, 1)
            v.tensor_copy(wg_t[:, :], ps_l1[0][:, P:2 * P]).then_inc(s_prep, 1)
            dve.wait_ge(s_gate_w, 1)
            v.tensor_copy(hg[:, 1], ps_l1[1][:, 0:P]).then_inc(s_prep, 1)
            dve.wait_ge(s_prep, 6)
            v.tensor_copy(hg_hi[:, :, :], hg[:, :, :]).then_inc(s_prep, 1)
            dve.wait_ge(s_prep, 7)
            v.tensor_tensor(hg_lo[:, :, :], hg[:, :, :], hg_hi[:, :, :].bitcast(F32), ALU.subtract).then_inc(s_prep, 1)
            v.tensor_copy(router_hi[:, :], raw_router[:, :]).then_inc(s_prep, 1)
            dve.wait_ge(s_prep, 9)
            v.tensor_tensor(router_lo[:, :], raw_router[:, :], router_hi[:, :].bitcast(F32), ALU.subtract)\
                .then_inc(s_prep, 1)
            dve.wait_ge(s_ident, 2)
            v.tensor_tensor(select[:, :, :],
                            ident[:, 0:EXPERTS].unsqueeze(2).to_broadcast([P, EXPERTS, P]),
                            ident[:, BLK:BLK + EXPERTS].unsqueeze(2).to_broadcast([P, EXPERTS, P]), ALU.add)\
                .then_inc(s_prep, 1)
            dve.wait_ge(s_w_loaded, DMA * N_BIG)
            for n in range(3):
                v.tensor_copy(w_hi[n][:, :, :], raw_w[n][:, :, :]).then_inc(s_prep, 1)
            v.tensor_copy(b3_split[:, :], raw_b3[:, :]).then_inc(s_prep, 1)
            dve.wait_ge(s_prep, 15)
            for n in range(3):
                v.tensor_tensor(w_lo[n][:, :, :], raw_w[n][:, :, :], w_hi[n][:, :, :].bitcast(F32), ALU.subtract)\
                    .then_inc(s_prep, 1)
            v.tensor_tensor(b3_split[2 * BLK:], raw_b3[2 * BLK:], b3_split[2 * BLK:].bitcast(F32), ALU.subtract)\
                .then_inc(s_prep, 1)
            dve.wait_ge(s_const, N_CONST)

        def dve_pipeline(dve, run):
            v = nc.vector
            gnn = run == 0

            def statistics(norm, g, c, s_ln):
                for b in range(GB):
                    last = v.bn_stats(stats[:, norm, b], X_of(g, b))
                last.then_inc(s_stats[norm], 1)
                wait_apart(dve, s_stats[norm], c + 1, s_ident)
                for b in range(GB):
                    last = v.bn_aggr(mean_var[:, norm, b], stats[:, norm, b])
                last.then_inc(s_mean_var[norm], 1)
                dve.wait_ge(s_mean_var[norm], c + 1)
                v.tensor_scalar(var_eps[:, norm], mean_var[:, norm, :, 1], LN_EPS, None, ALU.add)\
                    .then_inc(s_ln, 1)

            def normalise(norm, g, c, s_rstd, s_xn):
                dve.wait_ge(s_rstd, c + 1)
                for b in range(GB):
                    last = v.tensor_scalar(xn[:, norm, b * P:(b + 1) * P], X_of(g, b), mean_var[:, norm, b, 0:1],
                                           rstd[:, norm, b:b + 1], ALU.subtract, ALU.mult)
                last.then_inc(s_xn, 1)

            def route(c, first, last):
                wide = [P, GB, EXPERTS]

                def bc(tile):
                    return tile[:, :].unsqueeze(2).to_broadcast(wide)

                R = {name: t[:, :, :] for name, t in rt.items()}
                steps = {
                    1: lambda: v.tensor_tensor(R["z"], ps_w[:, 0:GB * EXPERTS].rearrange("p (b e) -> p b e", b=GB),
                                               logit_bias[:, :, :], ALU.add),
                    2: lambda: v.tensor_reduce(rc["max"][:, :], R["z"], AX.X, ALU.max),
                    3: lambda: v.tensor_tensor(R["shifted"], R["z"], bc(rc["max"]), ALU.subtract),
                    4: lambda: v.tensor_reduce(rc["sum"][:, :], R["exp"], AX.X, ALU.add),
                    5: lambda: v.reciprocal(rc["rsum"][:, :], rc["sum"][:, :]),
                    6: lambda: v.tensor_tensor(R["p"], R["exp"], bc(rc["rsum"]), ALU.mult),
                    7: lambda: v.tensor_reduce(rc["p1"][:, :], R["p"], AX.X, ALU.max),
                    8: lambda: v.tensor_tensor(R["hit"], R["p"], bc(rc["p1"]), ALU.is_equal),
                    9: lambda: v.tensor_tensor(R["rank"], R["hit"], priority[:, :, :], ALU.mult),
                    10: lambda: v.tensor_reduce(rc["best1"][:, :], R["rank"], AX.X, ALU.max),
                    11: lambda: v.tensor_tensor(R["first"], R["rank"], bc(rc["best1"]), ALU.is_equal),
                    12: lambda: v.scalar_tensor_tensor(R["rest"], R["first"], -4.0, R["p"], ALU.mult, ALU.add),
                    13: lambda: v.tensor_reduce(rc["p2"][:, :], R["rest"], AX.X, ALU.max),
                    14: lambda: v.tensor_tensor(R["hit"], R["rest"], bc(rc["p2"]), ALU.is_equal),
                    15: lambda: v.tensor_tensor(R["rank"], R["hit"], priority[:, :, :], ALU.mult),
                    16: lambda: v.tensor_reduce(rc["best2"][:, :], R["rank"], AX.X, ALU.max),
                    17: lambda: v.tensor_tensor(R["second"], R["rank"], bc(rc["best2"]), ALU.is_equal),
                    18: lambda: v.tensor_tensor(rc["gap"][:, :], rc["p1"][:, :], rc["p2"][:, :], ALU.subtract),
                    19: lambda: v.tensor_tensor(R["both"], R["first"], R["second"], ALU.add),
                    20: lambda: v.tensor_tensor(R["diff"], R["first"], R["second"], ALU.subtract),
                    21: lambda: v.scalar_tensor_tensor(R["tilt"], R["diff"], 0.5, bc(rc["tanh"]), ALU.mult, ALU.mult),
                    22: lambda: v.scalar_tensor_tensor(R["w"], R["both"], 0.5, R["tilt"], ALU.mult, ALU.add),
                    23: lambda: v.tensor_copy(w_blocks[:, :, 0:4:2, 0:EXPERTS],
                                              R["w"].unsqueeze(2).to_broadcast([P, GB, 2, EXPERTS])),
                    24: lambda: v.tensor_tensor(w_blocks[:, :, 1:4:2, 0:EXPERTS],
                                                R["w"].unsqueeze(2).to_broadcast([P, GB, 2, EXPERTS]),
                                                w_blocks_f[:, :, 0:4:2, 0:EXPERTS], ALU.subtract),
                }
                for t in range(first, last + 1):
                    if t == 1:
                        dve.wait_ge(s_logits, c + 1)
                    if t == 4:
                        dve.wait_ge(s_route_act, 2 * c + 1)
                    if t == 21:
                        dve.wait_ge(s_route_act, 2 * c + 2)
                    if t == 23:
                        wait(dve, s_w_t, c)
                    if t not in (4, 19, 20):
                        wait(dve, s_route, ROUTE * c + t - 1)
                    steps[t]().then_inc(s_route, 1)

            def iteration(i, n, parity):
                for s in range(STEPS):
                    if s == 0 and gnn and live(i + 1):
                        dve.wait_ge(s_xg_hi, n + 2)
                        v.tensor_tensor(xg_lo[:, :], ps_a, xg_hi[:, :].bitcast(F32), ALU.subtract)\
                            .then_inc(s_xg_lo, 1)
                    if s == 1 and gnn and live(i + 1):
                        dve.wait_ge(s_gate, n + 2)
                        wait(dve, s_vals_lo, n + 1)
                        wait(dve, s_vals_hi, n + 1)
                        v.scalar_tensor_tensor(vals[:, :, :], gate[:, :, :], 1.0, ps_hg[:, :, 0:P],
                                               ALU.add, ALU.mult).then_inc(s_vals, 1)
                    if s == 1 and live(i):
                        route(n, 1, 3)
                    if s == 2 and live(i):
                        route(n, 19, ROUTE)
                    if s == 3 and gnn and live(i + 1):
                        dve.wait_ge(s_agg, n + 2)
                        v.scalar_tensor_tensor(X_of(i + 1), ps_a, 0.0, X_of(i + 1), ALU.max, ALU.add)\
                            .then_inc(s_x1, 1)
                    if s == 3 and live(i + 1):
                        wait_apart(dve, s_xn2, n + 1, s_ident)
                        if gnn:
                            dve.wait_ge(s_x1, n + 2)
                        statistics(1, i + 1, n + 1, s_ln2)
                    if s == 4 and live(i + 1):
                        wait(dve, s_t2, n + 1)
                        normalise(1, i + 1, n + 1, s_rstd2, s_xn2)
                    if s == 5 and live(i + 1):
                        dve.wait_ge(s_xf_hi, n + 2)
                        v.tensor_tensor(xf_lo[:, 1 - parity], ps_a, xf_hi[:, 1 - parity].bitcast(F32), ALU.subtract)\
                            .then_inc(s_xf_lo, 1)
                    if live(i if s >= L2_LAG else i - 1):
                        k = EXPERTS * n + s - L2_LAG
                        dve.wait_ge(s_u2, k + 1)
                        dve.wait_ge(s_wb, k + 1)
                        wait(dve, s_r2_lo, k - 1)
                        v.tensor_tensor(v2[:, s % 2], u2[:, s % 2], ps_w[:, :], ALU.mult).then_inc(s_v2, 1)
                        dve.wait_ge(s_v2, k + 1)
                        wait(dve, s_l3, k + 1 - R2_RING)
                        v.tensor_copy(r2_hi[:, s % R2_RING], v2[:, s % 2]).then_inc(s_r2_hi, 1)
                    if s == 4 and isinstance(i, int) and i == GROUPS - 1 and gnn:
                        dve.wait_ge(s_over_sum, 1)
                        v.tensor_scalar(flag[:, :], ps_a[0:1, 0:1], 0.0, None, ALU.is_gt).then_inc(s_flag, 1)
                    if s == 0 and gnn and live(i + 1):
                        dve.wait_ge(s_adj_loaded[1 - parity], loads(i + 1))
                        wait(dve, s_agg, n + 1)
                        v.tensor_scalar(loop_edges[:, :], adj_in[:, 1 - parity], 1.0, None, ALU.is_equal)\
                            .then_inc(s_edges, 1)
                        dve.wait_ge(s_over, n + 2)
                        wait(dve, s_over_all, n + 1)
                        v.tensor_tensor(over_all[:, :], over_all[:, :], over_sum[:, 1 - parity:2 - parity], ALU.max)\
                            .then_inc(s_over_all, 1)
                    if s == 1 and gnn and live(i + 1):
                        dve.wait_ge(s_vals_hi, n + 2)
                        wait(dve, s_agg, n + 1)
                        v.tensor_tensor(tok3(vals_lo[:, :]), vals[:, :, :], tok3(vals_hi[:, :]).bitcast(F32),
                                        ALU.subtract).then_inc(s_vals_lo, 1)
                    if s == 1 and live(i):
                        route(n, 4, 18)
                    if s == 2 and gnn and live(i + 2):
                        wait_apart(dve, s_xn1, n + 2, s_ident)
                        dve.wait_ge(s_x_loaded[parity], loads(i + 2))
                        statistics(0, i + 2, n + 2, s_ln1)
                    if s == 4 and gnn and live(i + 2):
                        wait(dve, s_t1, n + 2)
                        normalise(0, i + 2, n + 2, s_rstd1, s_xn1)
                    if s == 5 and live(i - 2):
                        dve.wait_ge(s_out_t, n - 1)
                        v.tensor_tensor(X_of(i - 2), ps_b, X_of(i - 2), ALU.add).then_inc(s_final, 1)

            pipeline(dve, iteration, run)

        def pe_setup(pe):
            t = nc.tensor
            pe.wait_ge(s_small_loaded, DMA * N_SMALL)
            pe.wait_ge(s_ident, 2)
            for n in range(2):
                t.transpose(ps_l1[0][:, n * P:(n + 1) * P], raw_loop[:, n], ident[:, :]).then_inc(s_loop_t, 1)
            pe.wait_ge(s_prep, 5)
            t.matmul(ps_l1[1][:, 0:P], raw_loop[:, 0], wg_t[:, :], start=True, stop=True).then_inc(s_gate_w, 1)
            pe.wait_ge(s_prep, N_PREP)
            pe.wait_ge(s_const, 2)

        def pe_pipeline(pe, run):
            t = nc.tensor
            gnn = run == 0

            def product(ps, w_hi_, w_lo_, x_hi, x_lo, start=True):
                t.matmul(ps, w_hi_, x_hi, start=start, stop=False)
                t.matmul(ps, w_lo_, x_hi, start=False, stop=False)
                return t.matmul(ps, w_hi_, x_lo, start=False, stop=True)

            def transpose4(ps, tile):
                for b in range(GB):
                    last = t.transpose(ps[:, b * P:(b + 1) * P], tile[:, b * P:(b + 1) * P], ident[:, :])
                return last

            def iteration(i, n, parity):
                for s in range(STEPS):
                    if live(i if s >= L2_LAG else i - 1):
                        e = (s - L2_LAG) % EXPERTS
                        k = EXPERTS * n + s - L2_LAG
                        r = (s - L2_LAG) % R1_RING
                        pe.wait_ge(s_r1_hi, k + 1)
                        pe.wait_ge(s_r1_lo, k + 1)
                        wait(pe, s_u2, k - 1)
                        product(ps_l2[s % 2][:, :], w_hi[1][:, e], w_lo[1][:, e], r1_hi[:, r], r1_lo[:, r])\
                            .then_inc(s_l2, 1)
                        wait(pe, s_v2, k)
                        if e == 0:
                            pe.wait_ge(s_w_rows, n + 1)
                        if s == 1 and live(i):
                            pe.wait_ge(s_route, ROUTE * n + 1)
                        t.matmul(ps_w[:, :], select[:, e], w_rows[:, :], start=True, stop=True).then_inc(s_wb, 1)
                    if live(i):
                        k = EXPERTS * n + s
                        if s == 0:
                            pe.wait_ge(s_xf_lo, n + 1)
                        wait(pe, s_u1, k - 1)
                        product(ps_l1[s % 2][:, :], w_hi[0][:, s], w_lo[0][:, s], xf_hi[:, parity], xf_lo[:, parity])\
                            .then_inc(s_l1, 1)
                    if live(i if s >= L3_LAG else i - 1):
                        e = (s - L3_LAG) % EXPERTS
                        k = EXPERTS * n + s - L3_LAG
                        r = (s - L3_LAG + L2_LAG) % R2_RING
                        if e == 0:
                            wait(pe, s_ffn_t, n)
                            t.matmul(ps_l3[:, :], b3_split[:, :], w_rows[:, :], start=True, stop=False)
                        pe.wait_ge(s_r2_lo, k + 1)
                        t.matmul(ps_l3[:, :], w_hi[2][:, e], r2_hi[:, r], start=False, stop=False)
                        t.matmul(ps_l3[:, :], w_lo[2][:, e], r2_hi[:, r], start=False, stop=False)
                        t.matmul(ps_l3[:, :], w_hi[2][:, e], r2_lo[:, r], start=False, stop=e == EXPERTS - 1)\
                            .then_inc(s_l3, 1)
                    if s == 0 and gnn and live(i + 1):
                        pe.wait_ge(s_xg_lo, n + 2)
                        wait(pe, s_router_h, n + 1)
                        for bank in range(2):
                            ps = ps_side[:, bank * TOK:(bank + 1) * TOK]
                            t.matmul(ps, ones[:, :], hg_bias[:, :, :, :].rearrange("p a b c -> p (a b c)"),
                                     start=True, stop=False)
                            for half in range(2):
                                b = 2 * bank + half
                                o = ps[:, half * 2 * P:(half + 1) * 2 * P]
                                x_hi, x_lo = (xg[:, b * P:(b + 1) * P] for xg in (xg_hi, xg_lo))
                                hi, lo = (h[:, :, :].rearrange("p a b -> p (a b)") for h in (hg_hi, hg_lo))
                                t.matmul(o, x_hi, hi, start=False, stop=False)
                                t.matmul(o, x_hi, lo, start=False, stop=False)
                                last = t.matmul(o, x_lo, hi, start=False, stop=half == 1)
                        last.then_inc(s_hg, 1)
                    if s == 0 and live(i):
                        pe.wait_ge(s_router_h, n + 1)
                        wait(pe, s_v2, EXPERTS * n - L2_LAG + 1)
                        for b in range(GB):
                            last = t.matmul(ps_w[:, b * EXPERTS:(b + 1) * EXPERTS], router_h[:, b * P:(b + 1) * P],
                                            logit_w[:, :], start=True, stop=True)
                        last.then_inc(s_logits, 1)
                    if s == 2 and gnn and live(i + 1):
                        pe.wait_ge(s_edges, n + 2)
                        pe.wait_ge(s_vals_lo, n + 2)
                        for b in range(GB):
                            o = slice(b * P, (b + 1) * P)
                            t.matmul(ps_a[:, o], loop_edges[:, o], vals_hi[:, o], start=True, stop=False)
                            last = t.matmul(ps_a[:, o], loop_edges[:, o], vals_lo[:, o], start=False, stop=True)
                        last.then_inc(s_agg, 1)
                    if s == 2 and live(i):
                        pe.wait_ge(s_route, ROUTE * (n + 1))
                        wait(pe, s_v2, EXPERTS * n)
                        transpose4(ps_w, w_parts[:, :, :].rearrange("p b c -> p (b c)")).then_inc(s_w_t, 1)
                    if s == 3 and isinstance(i, int) and i == GROUPS - 1 and gnn:
                        pe.wait_ge(s_over_all, GROUPS)
                        t.matmul(ps_a[0:1, 0:1], over_all[:, :], ones[:, 0:1].bitcast(F32), start=True, stop=True)\
                            .then_inc(s_over_sum, 1)
                    if s == 3 and live(i - 2):
                        pe.wait_ge(s_ffn_t, n - 1)
                        if not live(i + 1):
                            wait(pe, s_final, n - 2)
                        transpose4(ps_b, ffn_t).then_inc(s_out_t, 1)
                    if s == 4 and live(i + 1):
                        pe.wait_ge(s_xn2, n + 2)
                        wait(pe, s_xf_lo, n + 1)
                        transpose4(ps_a, xn[:, 1]).then_inc(s_t2, 1)
                    if s == 5 and live(i + 1):
                        pe.wait_ge(s_xf_lo, n + 2)
                        wait(pe, s_final, n - 1)
                        product(ps_b, router_hi[:, :], router_lo[:, :], xf_hi[:, 1 - parity], xf_lo[:, 1 - parity])\
                            .then_inc(s_rh, 1)
                    if s == 5 and gnn and live(i + 2):
                        pe.wait_ge(s_xn1, n + 3)
                        wait(pe, s_xf_lo, n + 2)
                        transpose4(ps_a, xn[:, 0]).then_inc(s_t1, 1)

            pipeline(pe, iteration, run)

        DIRECTIONS = [
            (w_fwd, wg_fwd, b_fwd, bg_fwd, RELS // REL_CHUNK, REL_CHUNK, True, 0),
            (w_bwd, wg_bwd, b_bwd, bg_bwd, RELS // REL_CHUNK, REL_CHUNK, False, RELS // REL_CHUNK * GRAPHS),
            (w_loop, wg_loop, b_loop, bg_loop, 1, 1, False, 2 * (RELS // REL_CHUNK) * GRAPHS),
        ]
        VISITS = (2 * (RELS // REL_CHUNK) + 1) * GRAPHS

        def visits(eng, direction, visit, per_chunk=None):
            chunks, before = DIRECTIONS[direction][4], DIRECTIONS[direction][7]
            with eng.Fori(0, chunks) as chunk:
                if per_chunk is not None:
                    per_chunk(chunk)
                with eng.Fori(0, GRAPHS) as graph:
                    visit(chunk, graph, chunk * GRAPHS + graph + before)

        def chunks_before(direction):
            return DIRECTIONS[direction][7] // GRAPHS

        def general_sp(sp):
            sp.wait_ge(s_final, GROUPS)
            sp.wait_ge(s_stored, DMA * GROUPS)
            for d, (w, wg, b, bg, chunks, rels, _, before) in enumerate(DIRECTIONS):
                wait(sp, s_gen_gate_w, d)
                sp.dma_start(raw_loop[:, 0], w).then_inc(s_gen_w_loaded, DMA)
                sp.dma_start(raw_loop[:, 1], wg).then_inc(s_gen_w_loaded, DMA)

                def per_chunk(chunk, b=b, bg=bg, rels=rels, before=before):
                    wait_apart(sp, s_gen_step, (chunk * GRAPHS + before) * GEN_STEPS + 1, s_zeroed)
                    for n, rows in enumerate((b, bg)):
                        sp.dma_start(gen_bias[:, n, 0:rels], rows[bass.ds(chunk * rels, rels), :].partition_broadcast(P))\
                            .then_inc(s_gen_bias, DMA)

                def visit(chunk, graph, v):
                    wait_apart(sp, s_gen_in, v * 2 + 1, s_zeroed)
                    sp.dma_start(gen_x[:, :], x[bass.ds(graph, 1)].rearrange("g p d -> p (g d)"))\
                        .then_inc(s_gen_loaded, DMA)
                    sp.dma_start(gen_adj[:, :], adj[bass.ds(graph, 1)].rearrange("g p n -> p (g n)"))\
                        .then_inc(s_gen_loaded, DMA)

                visits(sp, d, visit, per_chunk)
            sp.wait_ge(s_gen_acc, VISITS + 1)
            with sp.Fori(0, GRAPHS) as graph:
                wait_apart(sp, s_gen_x1, graph + 1, s_zeroed)
                sp.dma_start(gen_x[:, :], x[bass.ds(graph, 1)].rearrange("g p d -> p (g d)"))\
                    .then_inc(s_gen_x_loaded, DMA)

        def general_pool(pool):
            pool.wait_ge(s_final, GROUPS)
            for r in range(RELS + 1):
                nc.gpsimd.memset(gen_number[:, r:r + 1], float(r + 1)).then_inc(s_gen_const, 1)

            def visit(chunk, graph, v):
                pool.wait_ge(s_gen_var, v + 1)
                nc.gpsimd.tensor_tensor(rstd[:, 0, 0:1], var_eps[:, 0, 0:1], minus_half[:, 0:1], ALU.pow)\
                    .then_inc(s_gen_rstd, 1)

            for d in range(3):
                visits(pool, d, visit)

        def general_act(act):
            act.wait_ge(s_final, GROUPS)
            for d, (_, _, _, _, _, rels, _, _) in enumerate(DIRECTIONS):
                def visit(chunk, graph, v, rels=rels):
                    act.wait_ge(s_gen_step, v * GEN_STEPS + 3)
                    nc.scalar.activation(gen_gate[:, 0:rels], gen_gate[:, 0:rels], ACT.Tanh, scale=0.5)\
                        .then_inc(s_gen_gate, 1)

                visits(act, d, visit)

        def general_pe(pe):
            t = nc.tensor
            pe.wait_ge(s_final, GROUPS)
            pe.sem_inc(s_gen_sum, 1)
            for d, (_, _, _, _, _, rels, turned, _) in enumerate(DIRECTIONS):
                pe.wait_ge(s_gen_w_loaded, DMA * 2 * (d + 1))
                pe.wait_ge(s_gen_acc, DIRECTIONS[d][7] + 1)
                for n in range(2):
                    last = t.transpose(ps_l1[0][:, n * P:(n + 1) * P], raw_loop[:, n], ident[:, :])
                last.then_inc(s_gen_w_t, 1)
                pe.wait_ge(s_gen_w, 3 * d + 2)
                t.matmul(ps_l1[1][:, 0:P], raw_loop[:, 0], wg_t[:, :], start=True, stop=True)\
                    .then_inc(s_gen_gate_w, 1)
                pe.wait_ge(s_gen_w, 3 * d + 3)

                def visit(chunk, graph, v, rels=rels, turned=turned):
                    pe.wait_ge(s_gen_in, v * 2 + 3)
                    last = t.transpose(ps_l1[0][:, 0:P], gen_xn[:, :], ident[:, :])
                    if turned:
                        last = t.transpose(ps_l1[0][:, P:2 * P], gen_rel[:, :], ident[:, :])
                    last.then_inc(s_gen_t, 1)
                    pe.wait_ge(s_gen_t_copied, v * 2 + 2)
                    t.matmul(ps_l1[1][:, 0:2 * P], gen_xn_t[:, :], gen_w[:, :, :].rearrange("p a b -> p (a b)"),
                             start=True, stop=True).then_inc(s_gen_hg, 1)
                    pe.wait_ge(s_gen_step, (v + 1) * GEN_STEPS + 1)
                    pe.wait_ge(s_gen_acc, v + 1)
                    for r in range(rels):
                        last = t.matmul(ps_l2[0][:, 0:P], gen_hot[:, r], gen_vals[:, r], start=r == 0, stop=r == rels - 1)
                    last.then_inc(s_gen_sum, 1)

                visits(pe, d, visit)

        def general_dve(dve):
            v_ = nc.vector
            dve.wait_ge(s_final, GROUPS)
            dve.wait_ge(s_stored, DMA * GROUPS)
            for counter in (s_gen_in, s_gen_step, s_gen_acc, s_gen_x1):
                dve.sem_inc(counter, 1)
            v_.memset(X[:, :], 0.0).then_inc(s_gen_const, 1)
            dve.wait_ge(s_gen_const, RELS + 2)
            for d, (_, _, _, _, _, rels, turned, _) in enumerate(DIRECTIONS):
                dve.wait_ge(s_gen_w_t, d + 1)
                wait(dve, s_gen_hg, DIRECTIONS[d][7])
                v_.tensor_copy(gen_w[:, 0], ps_l1[0][:, 0:P]).then_inc(s_gen_w, 1)
                v_.tensor_copy(wg_t[:, :], ps_l1[0][:, P:2 * P]).then_inc(s_gen_w, 1)
                dve.wait_ge(s_gen_gate_w, d + 1)
                v_.tensor_copy(gen_w[:, 1], ps_l1[1][:, 0:P]).then_inc(s_gen_w, 1)
                big = [P, rels, P]

                def visit(chunk, graph, v, rels=rels, turned=turned, big=big, d=d):
                    node = X[:, bass.ds(graph * P, P)]
                    wait_apart(dve, s_gen_loaded, (v + 1) * 2 * DMA, s_ident)
                    v_.bn_stats(stats[:, 0, 0], gen_x[:, :]).then_inc(s_gen_stats, 1)
                    wait_apart(dve, s_gen_stats, v + 1, s_ident)
                    v_.bn_aggr(mean_var[:, 0, 0], stats[:, 0, 0]).then_inc(s_gen_mean, 1)
                    dve.wait_ge(s_gen_mean, v + 1)
                    v_.tensor_scalar(var_eps[:, 0, 0:1], mean_var[:, 0, 0, 1:2], LN_EPS, None, ALU.add)\
                        .then_inc(s_gen_var, 1)
                    dve.wait_ge(s_gen_rstd, v + 1)
                    v_.tensor_scalar(gen_xn[:, :], gen_x[:, :], mean_var[:, 0, 0, 0:1], rstd[:, 0, 0:1],
                                     ALU.subtract, ALU.mult).then_inc(s_gen_in, 1)
                    dve.wait_ge(s_gen_step, v * GEN_STEPS + 1)
                    v_.tensor_copy(gen_rel[:, :], gen_adj[:, :]).then_inc(s_gen_in, 1)
                    dve.wait_ge(s_gen_t, v + 1)
                    v_.tensor_copy(gen_xn_t[:, :], ps_l1[0][:, 0:P]).then_inc(s_gen_t_copied, 1)
                    rel = gen_rel_t if turned else gen_rel
                    if turned:
                        v_.tensor_copy(gen_rel_t[:, :], ps_l1[0][:, P:2 * P]).then_inc(s_gen_t_copied, 1)
                    else:
                        v_.tensor_copy(gen_rel_t[:, :], gen_rel[:, :]).then_inc(s_gen_t_copied, 1)
                    dve.wait_ge(s_gen_hg, v + 1)
                    v_.tensor_copy(gen_hg[:, :, :], ps_l1[1][:, 0:2 * P].rearrange("p (a b) -> p a b", a=2))\
                        .then_inc(s_gen_step, 1)
                    dve.wait_ge(s_gen_step, v * GEN_STEPS + 2)
                    dve.wait_ge(s_gen_bias, (chunk + chunks_before(d) + 1) * 2 * DMA)
                    v_.tensor_tensor(gen_gate[:, 0:rels], gen_bias[:, 1, 0:rels],
                                     gen_hg[:, 1].unsqueeze(1).to_broadcast(big), ALU.add).then_inc(s_gen_step, 1)
                    dve.wait_ge(s_gen_sum, v + 1)
                    v_.tensor_tensor(gen_vals[:, 0:rels], gen_bias[:, 0, 0:rels],
                                     gen_hg[:, 0].unsqueeze(1).to_broadcast(big), ALU.add).then_inc(s_gen_step, 1)
                    numbers = gen_number[:, 0:1] if d == 2 else gen_number[:, bass.ds(chunk * rels + 1, rels)]
                    dve.wait_ge(s_gen_t_copied, v * 2 + 2)
                    v_.tensor_tensor(gen_hot[:, 0:rels], rel[:, :].unsqueeze(1).to_broadcast(big),
                                     numbers.unsqueeze(2).to_broadcast(big), ALU.is_equal).then_inc(s_gen_step, 1)
                    dve.wait_ge(s_gen_gate, v + 1)
                    dve.wait_ge(s_gen_step, v * GEN_STEPS + 5)
                    v_.scalar_tensor_tensor(gen_vals[:, 0:rels], gen_gate[:, 0:rels], 1.0, gen_vals[:, 0:rels],
                                            ALU.add, ALU.mult).then_inc(s_gen_step, 1)
                    dve.wait_ge(s_gen_sum, v + 2)
                    dve.wait_ge(s_gen_acc, v + 1)
                    v_.scalar_tensor_tensor(node, ps_l2[0][:, 0:P], 0.5, node, ALU.mult, ALU.add)\
                        .then_inc(s_gen_acc, 1)

                visits(dve, d, visit)
            dve.wait_ge(s_gen_acc, VISITS + 1)
            with dve.Fori(0, GRAPHS) as graph:
                node = X[:, bass.ds(graph * P, P)]
                dve.wait_ge(s_gen_x_loaded, (graph + 1) * DMA)
                v_.scalar_tensor_tensor(node, node, 0.0, gen_x[:, :], ALU.max, ALU.add).then_inc(s_gen_x1, 1)
            dve.wait_ge(s_gen_x1, GRAPHS + 1)

        def if_general(eng, general, again):
            eng.wait_ge(s_flag, 1)
            found = eng.value_load(flag[0:1, 0:1], min_val=0, max_val=1)
            with eng.If_ne(eng.to_reg(found), 0):
                general(eng)
                again(eng, 1)

        with nc.Block() as block:
            @block.sync
            def _(sp):
                sp_pipeline(sp, 0)
                if_general(sp, general_sp, sp_pipeline)

            @block.gpsimd
            def _(pool):
                pool_constants(pool)
                pool_pipeline(pool, 0)
                if_general(pool, general_pool, pool_pipeline)

            @block.scalar
            def _(act):
                act_pipeline(act, 0)
                if_general(act, general_act, act_pipeline)

            @block.vector
            def _(dve):
                dve_setup(dve)
                dve_pipeline(dve, 0)
                if_general(dve, general_dve, dve_pipeline)

            @block.tensor
            def _(pe):
                pe_setup(pe)
                pe_pipeline(pe, 0)
                if_general(pe, general_pe, pe_pipeline)


_INS = ['x', 'adj'] + ['L0_gnn_' + n for n in (
    'W_fwd', 'W_bwd', 'W_loop', 'Wg_fwd', 'Wg_bwd', 'Wg_loop', 'b_fwd', 'b_bwd', 'b_loop', 'bg_fwd', 'bg_bwd',
    'bg_loop')] + ['L0_ffn_' + n for n in (
        'router_w1', 'router_b1', 'router_w2', 'router_b2', 'expert_w1', 'expert_b1', 'expert_w2', 'expert_b2',
        'expert_w3', 'expert_b3')]


def kernel(**inputs):
    import numpy as _np
    import concourse.bacc as _bacc
    from concourse.bass_utils import run_bass_kernel_spmd as _run

    nc = _bacc.Bacc("TRN2", target_bir_lowering=False, num_devices=1)
    arrays, args = {}, []
    for name in _INS:
        a = _np.ascontiguousarray(inputs[name])
        arrays[f"in_{name}_dram"] = a
        args.append(nc.dram_tensor(f"in_{name}_dram", a.shape, mybir.dt.from_np(a.dtype), kind="ExternalInput").ap())
    out = nc.dram_tensor("out_0_dram", (GRAPHS, P, P), F32, kind="ExternalOutput").ap()
    adj_ffn_kernel(nc, *args, out)
    r = _run(nc, [arrays], core_ids=[0])
    return r.results[0]["out_0_dram"]
```

```python
from contextlib import ExitStack

import concourse.bass as bass
from concourse import mybir

F32 = mybir.dt.float32
F32R = mybir.dt.float32r
I32 = mybir.dt.int32
ALU = mybir.AluOpType
ACT = mybir.ActivationFunctionType
AX = mybir.AxisListType

P = 128
GRAPHS = 64
GB = 4
TOK = GB * P
GROUPS = GRAPHS // GB
EXPERTS = 6
STEPS = EXPERTS
ROUTER_H = 64
RELS = 39
REL_CHUNK = 13
L2_LAG = 6
L3_LAG = 8
R1_RING = 6
R2_RING = 3
LN_EPS = 1e-5
BLK = 32
DMA = 16


def wait(eng, sem, value):
    if not (isinstance(value, int) and value <= 0):
        eng.wait_ge(sem, value)


def wait_apart(eng, sem, value, reached):
    if not isinstance(value, int):
        value = eng.snap(eng.to_reg(value))
    eng.wait_ge(reached, 1)
    wait(eng, sem, value)


def live(g):
    return not isinstance(g, int) or 0 <= g < GROUPS


def group_at(i, s, lag):
    return i + (s - lag) // EXPERTS


def pipeline(eng, iteration, run=0, ahead=3):
    last = (GROUPS - ahead) // 2
    for i in range(-3, 2):
        iteration(i, i + GROUPS * run, i % 2)
    with eng.Fori(1, last) as pair:
        for parity in range(2):
            i = pair * 2 + parity
            iteration(i, i + GROUPS * run, parity)
    for i in range(2 * last, GROUPS + 2):
        iteration(i, i + GROUPS * run, i % 2)


def adj_ffn_kernel(nc, x, adj, w_fwd, w_bwd, w_loop, wg_fwd, wg_bwd, wg_loop, b_fwd, b_bwd, b_loop,
                   bg_fwd, bg_bwd, bg_loop, router_w1, router_b1, router_w2, router_b2,
                   expert_w1, expert_b1, expert_w2, expert_b2, expert_w3, expert_b3, out):
    with ExitStack() as ctx:
        ctx.enter_context(nc.allow_non_contiguous_dma(reason="bias columns and rows of tokens"))

        def sb(name, shape, dt=F32):
            return ctx.enter_context(nc.sbuf_tensor(name, shape, dt))

        def sem(name):
            return ctx.enter_context(nc.semaphore(name))

        ident = sb("ident", [P, P])
        raw_w = [sb(f"raw_w{n}", [P, EXPERTS, P]) for n in range(3)]
        w_hi = [sb(f"w_hi{n}", [P, EXPERTS, P], F32R) for n in range(3)]
        w_lo = [sb(f"w_lo{n}", [P, EXPERTS, P], F32R) for n in range(3)]
        bias2 = sb("bias2", [P, EXPERTS])
        raw_b3 = sb("raw_b3", [P, P])
        b3_split = sb("b3_split", [P, P], F32R)
        select = sb("select", [P, EXPERTS, P], F32R)
        raw_b1 = sb("raw_b1", [P, EXPERTS, P])
        raw_router = sb("raw_router", [P, P])
        raw_router_b = sb("raw_router_b", [P, P])
        router_hi = sb("router_hi", [P, P], F32R)
        router_lo = sb("router_lo", [P, P], F32R)
        logit_w = sb("logit_w", [P, EXPERTS])
        logit_bias = sb("logit_bias", [P, EXPERTS])
        priority = sb("priority", [P, GB, EXPERTS])
        minus_half = sb("minus_half", [P, GB])
        raw_loop = sb("raw_loop", [P, 2, P])
        wg_t = sb("wg_t", [P, P])
        hg = sb("hg", [P, 2, P])
        hg_hi = sb("hg_hi", [P, 2, P], F32R)
        hg_lo = sb("hg_lo", [P, 2, P], F32R)
        raw_hg_b = sb("raw_hg_b", [P, 2, P])
        ones = sb("ones", [P, P])

        X = sb("X", [P, GROUPS * TOK])
        adj_in = sb("adj_in", [P, 2, TOK], I32)
        loop_edges = sb("loop_edges", [P, TOK], F32R)
        over_one = sb("over_one", [P, TOK])
        over_sum = sb("over_sum", [P, 2])
        over_all = sb("over_all", [P, 1])
        minus_one = sb("minus_one", [P, 1])
        stats = sb("stats", [P, 2, GB, 6])
        mean_var = sb("mean_var", [P, 2, GB, 2])
        var_eps = sb("var_eps", [P, 2, GB])
        rstd = sb("rstd", [P, 2, GB])
        spread = sb("spread", [P, 2, GB])
        centre = sb("centre", [P, 2, GB])
        xn = sb("xn", [P, 2, TOK])
        xg_hi = sb("xg_hi", [P, TOK], F32R)
        xg_lo = sb("xg_lo", [P, TOK], F32R)
        gate = sb("gate", [P, GB, P])
        vals = sb("vals", [P, GB, P])
        vals_hi = sb("vals_hi", [P, TOK], F32R)
        vals_lo = sb("vals_lo", [P, TOK], F32R)
        xf_hi = sb("xf_hi", [P, 2, TOK], F32R)
        xf_lo = sb("xf_lo", [P, 2, TOK], F32R)
        router_h = sb("router_h", [P, TOK])
        rt = {n: sb("rt_" + n, [P, GB, EXPERTS]) for n in
              ("z", "shifted", "exp", "p", "rest", "hit", "rank", "first", "second", "both", "diff", "tilt", "w")}
        rc = {n: sb("rc_" + n, [P, GB]) for n in
              ("max", "sum", "rsum", "p1", "p2", "best1", "best2", "gap", "tanh")}
        w_parts = sb("w_parts", [P, GB, P])
        w_blocks_f = w_parts[:, :, :].rearrange("p b (q c) -> p b q c", c=BLK)
        w_blocks = w_parts[:, :, :].bitcast(F32R).rearrange("p b (q c) -> p b q c", c=BLK)
        w_rows = sb("w_rows", [P, TOK], F32R)
        r1_hi = sb("r1_hi", [P, R1_RING, TOK], F32R)
        r1_lo = sb("r1_lo", [P, R1_RING, TOK], F32R)
        u2 = sb("u2", [P, 2, TOK])
        v2 = sb("v2", [P, 2, TOK])
        r2_hi = sb("r2_hi", [P, R2_RING, TOK], F32R)
        r2_lo = sb("r2_lo", [P, R2_RING, TOK], F32R)
        ffn_t = sb("ffn_t", [P, TOK])

        flag = sb("flag", [1, 1], I32)
        gen_x = sb("gen_x", [P, P])
        gen_adj = sb("gen_adj", [P, P], I32)
        gen_xn = sb("gen_xn", [P, P])
        gen_xn_t = sb("gen_xn_t", [P, P])
        gen_rel = sb("gen_rel", [P, P])
        gen_rel_t = sb("gen_rel_t", [P, P])
        gen_hg = sb("gen_hg", [P, 2, P])
        gen_w = sb("gen_w", [P, 2, P])
        gen_bias = sb("gen_bias", [P, 2, REL_CHUNK, P])
        gen_vals = sb("gen_vals", [P, REL_CHUNK, P])
        gen_gate = sb("gen_gate", [P, REL_CHUNK, P])
        gen_hot = sb("gen_hot", [P, REL_CHUNK, P])
        gen_number = sb("gen_number", [P, RELS + 1])

        ps_l1 = [ctx.enter_context(nc.psum_tensor(f"ps_l1_{n}", [P, TOK], F32)) for n in range(2)]
        ps_l2 = [ctx.enter_context(nc.psum_tensor(f"ps_l2_{n}", [P, TOK], F32)) for n in range(2)]
        ps_l3 = ctx.enter_context(nc.psum_tensor("ps_l3", [P, TOK], F32))
        ps_w = ctx.enter_context(nc.psum_tensor("ps_w", [P, TOK], F32))
        ps_side = ctx.enter_context(nc.psum_tensor("ps_side", [P, 2 * TOK], F32))
        ps_a, ps_b = ps_side[:, 0:TOK], ps_side[:, TOK:2 * TOK]
        ps_hg = ps_side[:, :].rearrange("p (b c) -> p b c", c=2 * P)

        s_w1_loaded = sem("s_w1_loaded")
        s_rest_loaded = sem("s_rest_loaded")
        s_hg_loaded = sem("s_hg_loaded")
        s_zeroed = sem("s_zeroed")
        s_ident = sem("s_ident")
        s_loop_t = sem("s_loop_t")
        s_gate_w = sem("s_gate_w")
        s_col_sums = sem("s_col_sums")
        s_prep_hg = sem("s_prep_hg")
        s_prep = sem("s_prep")
        s_const = sem("s_const")
        s_x_loaded = [sem(f"s_x_loaded{n}") for n in range(2)]
        s_adj_loaded = [sem(f"s_adj_loaded{n}") for n in range(2)]
        s_stored = sem("s_stored")
        s_stats = [sem(f"s_stats{n}") for n in range(2)]
        s_mean_var = [sem(f"s_mean_var{n}") for n in range(2)]
        s_ln1 = sem("s_ln1")
        s_rstd1 = sem("s_rstd1")
        s_xn1 = sem("s_xn1")
        s_t1 = sem("s_t1")
        s_xg_hi = sem("s_xg_hi")
        s_xg_lo = sem("s_xg_lo")
        s_hg = sem("s_hg")
        s_gate = sem("s_gate")
        s_vals = sem("s_vals")
        s_vals_hi = sem("s_vals_hi")
        s_vals_lo = sem("s_vals_lo")
        s_edges = sem("s_edges")
        s_over = sem("s_over")
        s_over_all = sem("s_over_all")
        s_agg = sem("s_agg")
        s_x1 = sem("s_x1")
        s_ln2 = sem("s_ln2")
        s_rstd2 = sem("s_rstd2")
        s_xn2 = sem("s_xn2")
        s_t2 = sem("s_t2")
        s_xf_hi = sem("s_xf_hi")
        s_xf_lo = sem("s_xf_lo")
        s_rh = sem("s_rh")
        s_router_h = sem("s_router_h")
        s_logits = sem("s_logits")
        s_route = sem("s_route")
        s_route_act = sem("s_route_act")
        s_w_t = sem("s_w_t")
        s_w_rows = sem("s_w_rows")
        s_l1 = sem("s_l1")
        s_r1_hi = sem("s_r1_hi")
        s_r1_lo = sem("s_r1_lo")
        s_l2 = sem("s_l2")
        s_wb = sem("s_wb")
        s_u2 = sem("s_u2")
        s_v2 = sem("s_v2")
        s_r2_hi = sem("s_r2_hi")
        s_r2_lo = sem("s_r2_lo")
        s_l3 = sem("s_l3")
        s_ffn_t = sem("s_ffn_t")
        s_out_t = sem("s_out_t")
        s_final = sem("s_final")
        s_over_sum = sem("s_over_sum")
        s_flag = sem("s_flag")
        s_gen_w_loaded = sem("s_gen_w_loaded")
        s_gen_w_t = sem("s_gen_w_t")
        s_gen_w = sem("s_gen_w")
        s_gen_gate_w = sem("s_gen_gate_w")
        s_gen_bias = sem("s_gen_bias")
        s_gen_const = sem("s_gen_const")
        s_gen_loaded = sem("s_gen_loaded")
        s_gen_stats = sem("s_gen_stats")
        s_gen_mean = sem("s_gen_mean")
        s_gen_var = sem("s_gen_var")
        s_gen_rstd = sem("s_gen_rstd")
        s_gen_in = sem("s_gen_in")
        s_gen_t = sem("s_gen_t")
        s_gen_t_copied = sem("s_gen_t_copied")
        s_gen_hg = sem("s_gen_hg")
        s_gen_step = sem("s_gen_step")
        s_gen_gate = sem("s_gen_gate")
        s_gen_sum = sem("s_gen_sum")
        s_gen_acc = sem("s_gen_acc")
        s_gen_x_loaded = sem("s_gen_x_loaded")
        s_gen_x1 = sem("s_gen_x1")
        GEN_STEPS = 5
        ROUTE = 24

        x_v = x.rearrange("(g b) p d -> p g b d", b=GB)
        adj_v = adj.rearrange("(g b) p n -> p g b n", b=GB)
        out_v = out.rearrange("(g b) p d -> p g b d", b=GB)

        def X_of(g, b=None):
            if b is None:
                return X[:, bass.ds(g * TOK, TOK)]
            return X[:, bass.ds(g * TOK + b * P, P)]

        def tok3(ap):
            return ap.rearrange("p (b d) -> p b d", b=GB)

        N_HG, N_W1, N_REST = 4, 6, 9
        N_PREP_HG = 7
        N_PREP_1, N_PREP = 8, 15
        N_CONST = 3 + EXPERTS + 2

        def loads(g):
            return DMA * (g // 2 + 1)


        def load_inputs(act):
            act.dma_start(raw_loop[:, 0], w_loop).then_inc(s_hg_loaded, DMA)
            act.dma_start(raw_loop[:, 1], wg_loop).then_inc(s_hg_loaded, DMA)
            act.dma_start(raw_hg_b[:, 0], b_loop[0].partition_broadcast(P)).then_inc(s_hg_loaded, DMA)
            act.dma_start(raw_hg_b[:, 1], bg_loop[0].partition_broadcast(P)).then_inc(s_hg_loaded, DMA)
            act.dma_start(raw_w[0][:, :, :], expert_w1.rearrange("e d f -> d e f")).then_inc(s_w1_loaded, DMA)
            act.dma_start(raw_b1[:, :, :], expert_b1.partition_broadcast(P)).then_inc(s_w1_loaded, DMA)
            for half in range(2):
                o = slice(half * ROUTER_H, (half + 1) * ROUTER_H)
                act.dma_start(raw_router[:, o], router_w1).then_inc(s_w1_loaded, DMA)
                act.dma_start(raw_router_b[:, o], router_b1.partition_broadcast(P)).then_inc(s_w1_loaded, DMA)
            for n, w in ((1, expert_w2), (2, expert_w3)):
                act.dma_start(raw_w[n][:, :, :], w.rearrange("e d f -> d e f")).then_inc(s_rest_loaded, DMA)
            act.dma_start(logit_bias[:, :], router_b2.partition_broadcast(P)).then_inc(s_rest_loaded, DMA)
            act.dma_start(bias2[:, :], expert_b2.rearrange("e h -> h e")).then_inc(s_rest_loaded, DMA)
            act.wait_ge(s_zeroed, 2)
            act.dma_start(logit_w[0:ROUTER_H], router_w2).then_inc(s_rest_loaded, DMA)
            for n in range(4):
                act.dma_start(raw_b3[n * BLK:n * BLK + EXPERTS], expert_b3).then_inc(s_rest_loaded, DMA)

        def sp_pipeline(sp, run):
            def load(g, parity):
                wait_apart(sp, s_ln1, g - 1, s_ident)
                wait(sp, s_edges, g - 1)
                wait(sp, s_over, g - 1)
                sp.dma_start(tok3(X_of(g)), x_v[:, bass.ds(g, 1)].rearrange("p g b d -> p (g b) d"))\
                    .then_inc(s_x_loaded[parity], DMA)
                sp.dma_start(tok3(adj_in[:, parity]), adj_v[:, bass.ds(g, 1)].rearrange("p g b d -> p (g b) d"))\
                    .then_inc(s_adj_loaded[parity], DMA)

            def iteration(i, n, parity):
                if run == 0 and live(i + 4):
                    load(i + 4, parity)
                if live(i - 2):
                    wait_apart(sp, s_final, n - 1, s_ident)
                    sp.dma_start(out_v[:, bass.ds(i - 2, 1)].rearrange("p g b d -> p (g b) d"), tok3(X_of(i - 2)))\
                        .then_inc(s_stored, DMA)

            if run == 0:
                sp.wait_ge(s_ident, 1)
                load(0, 0)
            pipeline(sp, iteration, run, ahead=4)
            sp.wait_ge(s_stored, DMA * GROUPS * (run + 1))

        def pool_constants(pool):
            nc.gpsimd.memset(ident[:, :], 0.0).then_inc(s_ident, 1)
            nc.gpsimd.memset(logit_w[:, :], 0.0).then_inc(s_zeroed, 1)
            nc.gpsimd.memset(raw_b3[:, :], 0.0).then_inc(s_zeroed, 1)
            pool.wait_ge(s_ident, 1)
            nc.gpsimd.affine_select(out=ident[:, :], in_=ident[:, :], compare_op=ALU.not_equal, fill=1.0,
                                    base=0, pattern=[[-1, P]], channel_multiplier=1).then_inc(s_ident, 1)
            nc.gpsimd.memset(minus_half[:, :], -0.5).then_inc(s_const, 1)
            nc.gpsimd.memset(ones[:, :], 1.0).then_inc(s_const, 1)
            nc.gpsimd.memset(w_parts[:, :, :], 0.0).then_inc(s_const, 1)
            for e in range(EXPERTS):
                nc.gpsimd.memset(priority[:, :, e:e + 1], float(EXPERTS - e)).then_inc(s_const, 1)
            nc.gpsimd.memset(minus_one[:, :], -1.0).then_inc(s_const, 1)
            nc.gpsimd.memset(over_all[:, :], 0.0).then_inc(s_const, 1)
            pool.wait_ge(s_const, 1)

        def pool_pipeline(pool, run):
            def rstd_of(norm, c, s_var, s_rstd, s_xn):
                pool.wait_ge(s_var, c + 1)
                wait(pool, s_xn, c)
                nc.gpsimd.tensor_tensor(rstd[:, norm], var_eps[:, norm], minus_half[:, :], ALU.pow)\
                    .then_inc(s_rstd, 1)
                pool.wait_ge(s_rstd, 3 * c + 1)
                nc.gpsimd.tensor_tensor(spread[:, norm], var_eps[:, norm], rstd[:, norm], ALU.mult)\
                    .then_inc(s_rstd, 1)
                pool.wait_ge(s_rstd, 3 * c + 2)
                nc.gpsimd.tensor_tensor(centre[:, norm], mean_var[:, norm, :, 0], spread[:, norm], ALU.subtract)\
                    .then_inc(s_rstd, 1)

            def iteration(i, n, parity):
                for s in range(STEPS):
                    if s == 2 and live(i + 1):
                        rstd_of(1, n + 1, s_ln2, s_rstd2, s_xn2)
                    if s == 4 and run == 0 and live(i + 2):
                        pool.wait_ge(s_vals_hi, n + 3)
                        wait(pool, s_agg, n + 2)
                        nc.gpsimd.tensor_tensor(tok3(vals_lo[:, :]), vals[:, :, :], tok3(vals_hi[:, :]).bitcast(F32),
                                                ALU.subtract).then_inc(s_vals_lo, 1)
                    if live(group_at(i, s, L2_LAG)):
                        k = EXPERTS * n + s - L2_LAG
                        r = s % R2_RING
                        pool.wait_ge(s_r2_hi, k + 1)
                        wait(pool, s_l3, k + 1 - R2_RING)
                        nc.gpsimd.tensor_tensor(r2_lo[:, r], v2[:, s % 2], r2_hi[:, r].bitcast(F32), ALU.subtract)\
                            .then_inc(s_r2_lo, 1)
                    if s == 5 and run == 0 and live(i + 3):
                        rstd_of(0, n + 3, s_ln1, s_rstd1, s_xn1)

            pipeline(pool, iteration, run)

        def act_pipeline(act, run):
            gnn = run == 0

            def iteration(i, n, parity):
                for s in range(STEPS):
                    if s == 0 and live(i - 1):
                        act.wait_ge(s_w_t, n)
                        nc.scalar.activation(w_rows[:, :], ps_a, ACT.Copy).then_inc(s_w_rows, 1)
                    if s == 1 and live(i):
                        act.wait_ge(s_rh, n + 1)
                        wait(act, s_logits, n)
                        nc.scalar.activation(router_h[:, :], ps_a, ACT.Relu).then_inc(s_router_h, 1)
                    if s == 2 and live(i - 2):
                        act.wait_ge(s_l3, EXPERTS * (n - 1))
                        nc.scalar.activation(ffn_t[:, :], ps_l3[:, :], ACT.Copy).then_inc(s_ffn_t, 1)
                    if s == 2 and gnn and live(i + 2):
                        act.wait_ge(s_t1, n + 3)
                        wait(act, s_hg, n + 2)
                        nc.scalar.activation(xg_hi[:, :], ps_b, ACT.Copy).then_inc(s_xg_hi, 1)
                    if s == 4 and gnn and live(i + 2):
                        act.wait_ge(s_hg, n + 3)
                        wait(act, s_vals, n + 2)
                        nc.scalar.activation(gate[:, :, :], ps_hg[:, :, P:2 * P], ACT.Tanh, scale=0.5)\
                            .then_inc(s_gate, 1)
                    if s == 5 and live(i + 1):
                        act.wait_ge(s_t2, n + 2)
                        wait(act, s_l1, EXPERTS * n)
                        nc.scalar.activation(xf_hi[:, 1 - parity], ps_a, ACT.Copy).then_inc(s_xf_hi, 1)
                    if live(group_at(i, s, L2_LAG)):
                        e = (s - L2_LAG) % EXPERTS
                        k = EXPERTS * n + s - L2_LAG
                        act.wait_ge(s_l2, k + 1)
                        wait(act, s_v2, k - 1)
                        nc.scalar.activation(u2[:, s % 2], ps_l2[s % 2][:, :], ACT.Relu, bias=bias2[:, e:e + 1])\
                            .then_inc(s_u2, 1)
                    if live(i):
                        k = EXPERTS * n + s
                        act.wait_ge(s_l1, k + 1)
                        wait(act, s_l2, k + 1 - R1_RING)
                        nc.scalar.activation(r1_hi[:, s], ps_l1[s % 2][:, :], ACT.Relu).then_inc(s_r1_hi, 1)
                    if s == 4 and gnn and live(i + 2):
                        act.wait_ge(s_vals, n + 3)
                        wait(act, s_agg, n + 2)
                        nc.scalar.activation(tok3(vals_hi[:, :]), vals[:, :, :], ACT.Copy).then_inc(s_vals_hi, 1)
                    if live(group_at(i, s, L2_LAG)):
                        k = EXPERTS * n + s - L2_LAG
                        act.wait_ge(s_v2, k + 1)
                        wait(act, s_l3, k + 1 - R2_RING)
                        nc.scalar.activation(r2_hi[:, s % R2_RING], v2[:, s % 2], ACT.Copy).then_inc(s_r2_hi, 1)
                    if s == 2 and live(i):
                        act.wait_ge(s_route, ROUTE * n + 3)
                        nc.scalar.activation(rt["exp"][:, :, :], rt["shifted"][:, :, :], ACT.Exp)\
                            .then_inc(s_route_act, 1)
                    if s == 3 and gnn and live(i + 2):
                        act.wait_ge(s_adj_loaded[parity], loads(i + 2))
                        wait(act, s_over, n + 2)
                        wait(act, s_over_all, n + 1)
                        nc.scalar.activation(over_one[:, :], adj_in[:, parity], ACT.Relu, bias=minus_one[:, :],
                                             accum_out=over_sum[:, parity:parity + 1]).then_inc(s_over, 1)
                    if s == 4 and live(i):
                        act.wait_ge(s_route, ROUTE * n + 18)
                        nc.scalar.activation(rc["tanh"][:, :], rc["gap"][:, :], ACT.Tanh, scale=0.5)\
                            .then_inc(s_route_act, 1)

            if run == 0:
                load_inputs(act)
                act.wait_ge(s_const, N_CONST)
                act.wait_ge(s_rest_loaded, DMA * N_REST)
            pipeline(act, iteration, run)

        def shift_and_split(dve, w, bias, ps, w_hi_, w_lo_, counter, done):
            nc.vector.tensor_tensor(bias, bias, ps, ALU.subtract).then_inc(counter, 1)
            dve.wait_ge(counter, done + 1)
            nc.vector.scalar_tensor_tensor(w, bias, 1.0 / P, w, ALU.mult, ALU.add).then_inc(counter, 1)
            dve.wait_ge(counter, done + 2)
            nc.vector.tensor_copy(w_hi_, w).then_inc(counter, 1)
            dve.wait_ge(counter, done + 3)
            nc.vector.tensor_tensor(w_lo_, w, w_hi_.bitcast(F32), ALU.subtract).then_inc(counter, 1)

        def prepare_hg(dve):
            v = nc.vector
            dve.wait_ge(s_hg_loaded, DMA * N_HG)
            dve.wait_ge(s_loop_t, 2)
            v.tensor_copy(wg_t[:, :], ps_l1[0][:, P:2 * P]).then_inc(s_prep_hg, 1)
            v.tensor_scalar(hg[:, 0], ps_l1[0][:, 0:P], 0.5, None, ALU.mult)
            v.tensor_scalar(raw_hg_b[:, 0], raw_hg_b[:, 0], 0.5, None, ALU.mult)
            dve.wait_ge(s_gate_w, 1)
            v.tensor_copy(hg[:, 1], ps_l1[1][:, 0:P]).then_inc(s_prep_hg, 2)
            dve.wait_ge(s_col_sums, 1)
            shift_and_split(dve, hg[:, :, :], raw_hg_b[:, :, :],
                            ps_l2[0][:, 0:2 * P].rearrange("p (a b) -> p a b", a=2),
                            hg_hi[:, :, :], hg_lo[:, :, :], s_prep_hg, 3)

        def prepare_first(dve):
            dve.wait_ge(s_w1_loaded, DMA * N_W1)
            dve.wait_ge(s_col_sums, 2)
            shift_and_split(dve, raw_router[:, :], raw_router_b[:, :], ps_w[:, 0:P], router_hi[:, :],
                            router_lo[:, :], s_prep, 0)
            half = EXPERTS // 2
            dve.wait_ge(s_col_sums, 3)
            for n in range(2):
                e = slice(n * half, (n + 1) * half)
                last = nc.vector.tensor_tensor(raw_b1[:, e], raw_b1[:, e],
                                               ps_l2[n][:, 0:half * P].rearrange("p (e f) -> p e f", e=half),
                                               ALU.subtract)
            last.then_inc(s_prep, 1)
            dve.wait_ge(s_prep, 5)
            nc.vector.scalar_tensor_tensor(raw_w[0][:, :, :], raw_b1[:, :, :], 1.0 / P, raw_w[0][:, :, :],
                                           ALU.mult, ALU.add).then_inc(s_prep, 1)
            dve.wait_ge(s_prep, 6)
            nc.vector.tensor_copy(w_hi[0][:, :, :], raw_w[0][:, :, :]).then_inc(s_prep, 1)
            dve.wait_ge(s_prep, 7)
            nc.vector.tensor_tensor(w_lo[0][:, :, :], raw_w[0][:, :, :], w_hi[0][:, :, :].bitcast(F32), ALU.subtract)\
                .then_inc(s_prep, 1)

        def prepare_rest(dve):
            v = nc.vector
            dve.wait_ge(s_rest_loaded, DMA * N_REST)
            for n in (1, 2):
                v.tensor_copy(w_hi[n][:, :, :], raw_w[n][:, :, :]).then_inc(s_prep, 1)
            v.tensor_copy(b3_split[:, :], raw_b3[:, :]).then_inc(s_prep, 1)
            v.tensor_tensor(select[:, :, :],
                            ident[:, 0:EXPERTS].unsqueeze(2).to_broadcast([P, EXPERTS, P]),
                            ident[:, BLK:BLK + EXPERTS].unsqueeze(2).to_broadcast([P, EXPERTS, P]), ALU.add)\
                .then_inc(s_prep, 1)
            dve.wait_ge(s_prep, N_PREP_1 + 4)
            for n in (1, 2):
                v.tensor_tensor(w_lo[n][:, :, :], raw_w[n][:, :, :], w_hi[n][:, :, :].bitcast(F32), ALU.subtract)\
                    .then_inc(s_prep, 1)
            v.tensor_tensor(b3_split[2 * BLK:], raw_b3[2 * BLK:], b3_split[2 * BLK:].bitcast(F32), ALU.subtract)\
                .then_inc(s_prep, 1)
            dve.wait_ge(s_const, N_CONST)

        def dve_pipeline(dve, run):
            v = nc.vector
            gnn = run == 0

            def statistics(norm, g, b):
                done = v.bn_stats(stats[:, norm, b], X_of(g, b))
                if b == GB - 1:
                    done.then_inc(s_stats[norm], 1)

            def aggregate(norm, c):
                wait_apart(dve, s_stats[norm], c + 1, s_ident)
                for b in range(GB):
                    last = v.bn_aggr(mean_var[:, norm, b], stats[:, norm, b])
                last.then_inc(s_mean_var[norm], 1)

            def add_eps(norm, c, s_ln):
                dve.wait_ge(s_mean_var[norm], c + 1)
                v.tensor_scalar(var_eps[:, norm], mean_var[:, norm, :, 1], LN_EPS, None, ALU.add)\
                    .then_inc(s_ln, 1)

            def normalise(norm, g, b, s_xn):
                done = v.tensor_scalar(xn[:, norm, b * P:(b + 1) * P], X_of(g, b), centre[:, norm, b:b + 1],
                                       rstd[:, norm, b:b + 1], ALU.subtract, ALU.mult)
                if b == GB - 1:
                    done.then_inc(s_xn, 1)

            def route(c, first, last):
                wide = [P, GB, EXPERTS]

                def bc(tile):
                    return tile[:, :].unsqueeze(2).to_broadcast(wide)

                R = {name: t[:, :, :] for name, t in rt.items()}
                steps = {
                    1: lambda: v.tensor_tensor(R["z"], ps_a[:, 0:GB * EXPERTS].rearrange("p (b e) -> p b e", b=GB),
                                               logit_bias[:, :].unsqueeze(1).to_broadcast(wide), ALU.add),
                    2: lambda: v.tensor_reduce(rc["max"][:, :], R["z"], AX.X, ALU.max),
                    3: lambda: v.tensor_tensor(R["shifted"], R["z"], bc(rc["max"]), ALU.subtract),
                    4: lambda: v.tensor_reduce(rc["sum"][:, :], R["exp"], AX.X, ALU.add),
                    5: lambda: v.reciprocal(rc["rsum"][:, :], rc["sum"][:, :]),
                    6: lambda: v.tensor_tensor(R["p"], R["exp"], bc(rc["rsum"]), ALU.mult),
                    7: lambda: v.tensor_reduce(rc["p1"][:, :], R["p"], AX.X, ALU.max),
                    8: lambda: v.tensor_tensor(R["hit"], R["p"], bc(rc["p1"]), ALU.is_equal),
                    9: lambda: v.tensor_tensor(R["rank"], R["hit"], priority[:, :, :], ALU.mult),
                    10: lambda: v.tensor_reduce(rc["best1"][:, :], R["rank"], AX.X, ALU.max),
                    11: lambda: v.tensor_tensor(R["first"], R["rank"], bc(rc["best1"]), ALU.is_equal),
                    12: lambda: v.scalar_tensor_tensor(R["rest"], R["first"], -4.0, R["p"], ALU.mult, ALU.add),
                    13: lambda: v.tensor_reduce(rc["p2"][:, :], R["rest"], AX.X, ALU.max),
                    14: lambda: v.tensor_tensor(R["hit"], R["rest"], bc(rc["p2"]), ALU.is_equal),
                    15: lambda: v.tensor_tensor(R["rank"], R["hit"], priority[:, :, :], ALU.mult),
                    16: lambda: v.tensor_reduce(rc["best2"][:, :], R["rank"], AX.X, ALU.max),
                    17: lambda: v.tensor_tensor(R["second"], R["rank"], bc(rc["best2"]), ALU.is_equal),
                    18: lambda: v.tensor_tensor(rc["gap"][:, :], rc["p1"][:, :], rc["p2"][:, :], ALU.subtract),
                    19: lambda: v.tensor_tensor(R["both"], R["first"], R["second"], ALU.add),
                    20: lambda: v.tensor_tensor(R["diff"], R["first"], R["second"], ALU.subtract),
                    21: lambda: v.scalar_tensor_tensor(R["tilt"], R["diff"], 0.5, bc(rc["tanh"]), ALU.mult, ALU.mult),
                    22: lambda: v.scalar_tensor_tensor(R["w"], R["both"], 0.5, R["tilt"], ALU.mult, ALU.add),
                    23: lambda: v.tensor_copy(w_blocks[:, :, 0:4:2, 0:EXPERTS],
                                              R["w"].unsqueeze(2).to_broadcast([P, GB, 2, EXPERTS])),
                    24: lambda: v.tensor_tensor(w_blocks[:, :, 1:4:2, 0:EXPERTS],
                                                R["w"].unsqueeze(2).to_broadcast([P, GB, 2, EXPERTS]),
                                                w_blocks_f[:, :, 0:4:2, 0:EXPERTS], ALU.subtract),
                }
                for t in range(first, last + 1):
                    if t == 1:
                        dve.wait_ge(s_logits, c + 1)
                    if t == 4:
                        dve.wait_ge(s_route_act, 2 * c + 1)
                    if t == 21:
                        dve.wait_ge(s_route_act, 2 * c + 2)
                    if t == 23:
                        wait(dve, s_w_t, c)
                    if t not in (4, 19, 20):
                        wait(dve, s_route, ROUTE * c + t - 1)
                    steps[t]().then_inc(s_route, 1)

            def iteration(i, n, parity):
                def weigh(s):
                    if live(group_at(i, s, L2_LAG)):
                        k = EXPERTS * n + s - L2_LAG
                        dve.wait_ge(s_u2, k + 1)
                        dve.wait_ge(s_wb, k + 1)
                        wait(dve, s_r2_lo, k - 1)
                        v.tensor_tensor(v2[:, s % 2], u2[:, s % 2], ps_w[:, :], ALU.mult).then_inc(s_v2, 1)

                def low_part(s):
                    if live(i):
                        k = EXPERTS * n + s
                        dve.wait_ge(s_r1_hi, k + 1)
                        v.scalar_tensor_tensor(r1_lo[:, s], ps_l1[s % 2][:, :], 0.0, r1_hi[:, s].bitcast(F32),
                                               ALU.max, ALU.subtract).then_inc(s_r1_lo, 1)

                def routing(first, last):
                    if live(i):
                        route(n, first, last)

                static = isinstance(i, int)

                if gnn and live(i + 1):
                    dve.wait_ge(s_agg, n + 2)
                    v.scalar_tensor_tensor(X_of(i + 1), ps_b, 0.0, X_of(i + 1), ALU.max, ALU.add)\
                        .then_inc(s_x1, 1)
                weigh(0)
                if live(i + 1):
                    wait_apart(dve, s_rstd2, 3 * (n + 1), s_ident)
                    if gnn:
                        dve.wait_ge(s_x1, n + 2)
                    for b in range(GB):
                        statistics(1, i + 1, b)
                low_part(0)
                if gnn and live(i + 2):
                    dve.wait_ge(s_rstd1, 3 * (n + 3))
                    wait(dve, s_t1, n + 2)
                    for b in range(GB):
                        normalise(0, i + 2, b, s_xn1)

                weigh(1)
                if live(i + 1):
                    aggregate(1, n + 1)
                low_part(1)
                if live(i + 1):
                    add_eps(1, n + 1, s_ln2)
                if gnn and live(i + 2):
                    dve.wait_ge(s_adj_loaded[parity], loads(i + 2))
                    wait(dve, s_agg, n + 2)
                    v.tensor_scalar(loop_edges[:, :], adj_in[:, parity], 1.0, None, ALU.is_equal)\
                        .then_inc(s_edges, 1)
                if run == 0 and static and i == -1:
                    prepare_rest(dve)

                if gnn and live(i + 2):
                    dve.wait_ge(s_xg_hi, n + 3)
                    v.tensor_tensor(xg_lo[:, :], ps_b, xg_hi[:, :].bitcast(F32), ALU.subtract).then_inc(s_xg_lo, 1)
                if run == 0 and static and i == -2:
                    prepare_first(dve)
                routing(1, 1)
                weigh(2)
                routing(2, 2)
                low_part(2)
                routing(3, 3)

                if live(i - 2):
                    dve.wait_ge(s_out_t, n - 1)
                    v.tensor_tensor(X_of(i - 2), ps_a, X_of(i - 2), ALU.add).then_inc(s_final, 1)
                routing(4, 4)
                weigh(3)
                routing(5, 5)
                low_part(3)
                routing(6, 6)
                if live(i + 1):
                    dve.wait_ge(s_rstd2, 3 * (n + 2))
                    wait(dve, s_t2, n + 1)
                for b in range(GB):
                    if live(i + 1):
                        normalise(1, i + 1, b, s_xn2)
                    routing(7 + b, 7 + b)

                if gnn and live(i + 2):
                    dve.wait_ge(s_gate, n + 3)
                    wait(dve, s_vals_lo, n + 2)
                    v.scalar_tensor_tensor(vals[:, :, :], gate[:, :, :], 1.0, ps_hg[:, :, 0:P], ALU.add, ALU.mult)\
                        .then_inc(s_vals, 1)
                routing(11, 11)
                weigh(4)
                routing(12, 12)
                low_part(4)
                routing(13, 13)
                if gnn and live(i + 3):
                    wait_apart(dve, s_rstd1, 3 * (n + 3), s_ident)
                    dve.wait_ge(s_x_loaded[1 - parity], loads(i + 3))
                for b in range(GB):
                    if gnn and live(i + 3):
                        statistics(0, i + 3, b)
                    routing(14 + b, 14 + b)
                if gnn and live(i + 2):
                    dve.wait_ge(s_over, n + 3)
                    wait(dve, s_over_all, n + 2)
                    v.tensor_tensor(over_all[:, :], over_all[:, :], over_sum[:, parity:parity + 1], ALU.max)\
                        .then_inc(s_over_all, 1)
                routing(18, 20)

                if live(i + 1):
                    dve.wait_ge(s_xf_hi, n + 2)
                    v.tensor_tensor(xf_lo[:, 1 - parity], ps_a, xf_hi[:, 1 - parity].bitcast(F32), ALU.subtract)\
                        .then_inc(s_xf_lo, 1)
                routing(21, 21)
                weigh(5)
                routing(22, 22)
                if gnn and live(i + 3):
                    aggregate(0, n + 3)
                routing(23, 23)
                low_part(5)
                routing(24, 24)
                if gnn and live(i + 3):
                    add_eps(0, n + 3, s_ln1)
                if static and i == GROUPS - 1 and gnn:
                    dve.wait_ge(s_over_sum, 1)
                    v.tensor_scalar(flag[:, :], ps_b[0:1, 0:1], 0.0, None, ALU.is_gt).then_inc(s_flag, 1)

            pipeline(dve, iteration, run)

        def pe_setup(pe):
            t = nc.tensor
            pe.wait_ge(s_hg_loaded, DMA * N_HG)
            pe.wait_ge(s_ident, 2)
            for n in range(2):
                t.transpose(ps_l1[0][:, n * P:(n + 1) * P], raw_loop[:, n], ident[:, :]).then_inc(s_loop_t, 1)
            pe.wait_ge(s_prep_hg, 1)
            t.matmul(ps_l1[1][:, 0:P], raw_loop[:, 0], wg_t[:, :], start=True, stop=True).then_inc(s_gate_w, 1)
            pe.wait_ge(s_const, 2)
            pe.wait_ge(s_prep_hg, 3)
            t.matmul(ps_l2[0][:, 0:2 * P], ones[:, :], hg[:, :, :].rearrange("p a b -> p (a b)"), start=True, stop=True)\
                .then_inc(s_col_sums, 1)

        def pe_column_sums(pe):
            t = nc.tensor
            pe.wait_ge(s_w1_loaded, DMA * N_W1)
            t.matmul(ps_w[:, 0:P], ones[:, :], raw_router[:, :], start=True, stop=True).then_inc(s_col_sums, 1)
            pe.wait_ge(s_prep_hg, N_PREP_HG)
            half = EXPERTS // 2
            for n in range(2):
                last = t.matmul(ps_l2[n][:, 0:half * P], ones[:, :],
                                raw_w[0][:, n * half:(n + 1) * half].rearrange("p e f -> p (e f)"),
                                start=True, stop=True)
            last.then_inc(s_col_sums, 1)

        def pe_pipeline(pe, run):
            t = nc.tensor
            gnn = run == 0

            def product(ps, w_hi_, w_lo_, x_hi, x_lo, start=True):
                t.matmul(ps, w_hi_, x_hi, start=start, stop=False)
                t.matmul(ps, w_lo_, x_hi, start=False, stop=False)
                return t.matmul(ps, w_hi_, x_lo, start=False, stop=True)

            def transpose4(ps, tile):
                for b in range(GB):
                    last = t.transpose(ps[:, b * P:(b + 1) * P], tile[:, b * P:(b + 1) * P], ident[:, :])
                return last

            def iteration(i, n, parity):
                static = isinstance(i, int)
                for s in range(STEPS):
                    if live(group_at(i, s, L2_LAG)):
                        e = (s - L2_LAG) % EXPERTS
                        k = EXPERTS * n + s - L2_LAG
                        r = (s - L2_LAG) % R1_RING
                        if run == 0 and static and k == 0:
                            pe.wait_ge(s_prep, N_PREP)
                        pe.wait_ge(s_r1_lo, k + 1)
                        wait(pe, s_u2, k - 1)
                        product(ps_l2[s % 2][:, :], w_hi[1][:, e], w_lo[1][:, e], r1_hi[:, r], r1_lo[:, r])\
                            .then_inc(s_l2, 1)
                    if s == 0 and live(i - 1):
                        pe.wait_ge(s_route, ROUTE * n)
                        if live(i):
                            pe.wait_ge(s_xf_lo, n + 1)
                        else:
                            wait(pe, s_final, n - 2)
                        transpose4(ps_a, w_parts[:, :, :].rearrange("p b c -> p (b c)")).then_inc(s_w_t, 1)
                    if live(i):
                        k = EXPERTS * n + s
                        if s == 0:
                            if run == 0 and static and i == 0:
                                pe.wait_ge(s_prep, N_PREP_1)
                            pe.wait_ge(s_xf_lo, n + 1)
                        wait(pe, s_r1_lo, k - 1)
                        product(ps_l1[s % 2][:, :], w_hi[0][:, s], w_lo[0][:, s], xf_hi[:, parity], xf_lo[:, parity])\
                            .then_inc(s_l1, 1)
                    if live(group_at(i, s, L3_LAG)):
                        e = (s - L3_LAG) % EXPERTS
                        k = EXPERTS * n + s - L3_LAG
                        r = (s - L3_LAG + L2_LAG) % R2_RING
                        if e == 0:
                            wait(pe, s_ffn_t, n - 1)
                            t.matmul(ps_l3[:, :], b3_split[:, :], w_rows[:, :], start=True, stop=False)
                        pe.wait_ge(s_r2_lo, k + 1)
                        t.matmul(ps_l3[:, :], w_hi[2][:, e], r2_hi[:, r], start=False, stop=False)
                        t.matmul(ps_l3[:, :], w_lo[2][:, e], r2_hi[:, r], start=False, stop=False)
                        t.matmul(ps_l3[:, :], w_hi[2][:, e], r2_lo[:, r], start=False, stop=e == EXPERTS - 1)\
                            .then_inc(s_l3, 1)
                    if live(group_at(i, s, L2_LAG)):
                        e = (s - L2_LAG) % EXPERTS
                        k = EXPERTS * n + s - L2_LAG
                        wait(pe, s_v2, k)
                        if e == 0:
                            pe.wait_ge(s_w_rows, n)
                        t.matmul(ps_w[:, :], select[:, e], w_rows[:, :], start=True, stop=True).then_inc(s_wb, 1)
                    if s == 0 and live(i):
                        if live(i - 1):
                            wait(pe, s_w_rows, n)
                        product(ps_a, router_hi[:, :], router_lo[:, :], xf_hi[:, parity], xf_lo[:, parity])\
                            .then_inc(s_rh, 1)
                    if s == 1 and live(i):
                        pe.wait_ge(s_router_h, n + 1)
                        for b in range(GB):
                            last = t.matmul(ps_a[:, b * EXPERTS:(b + 1) * EXPERTS], router_h[:, b * P:(b + 1) * P],
                                            logit_w[:, :], start=True, stop=True)
                        last.then_inc(s_logits, 1)
                    if s == 1 and gnn and live(i + 2):
                        pe.wait_ge(s_xn1, n + 3)
                        wait(pe, s_x1, n + 2)
                        transpose4(ps_b, xn[:, 0]).then_inc(s_t1, 1)
                        if static and i == -2:
                            pe_column_sums(pe)
                    if s == 2 and live(i - 2):
                        pe.wait_ge(s_ffn_t, n - 1)
                        if live(i):
                            pe.wait_ge(s_route, ROUTE * n + 1)
                        else:
                            wait(pe, s_w_rows, GROUPS * (run + 1))
                            wait(pe, s_final, n - 2)
                        transpose4(ps_a, ffn_t).then_inc(s_out_t, 1)
                    if s == 3 and gnn and live(i + 2):
                        pe.wait_ge(s_xg_lo, n + 3)
                        if not live(i):
                            pe.wait_ge(s_prep_hg, N_PREP_HG)
                        elif not live(i - 2):
                            pe.wait_ge(s_route, ROUTE * n + 1)
                        else:
                            pe.wait_ge(s_final, n - 1)
                        hi, lo = (h[:, :, :].rearrange("p a b -> p (a b)") for h in (hg_hi, hg_lo))
                        for b in range(GB):
                            o = slice(b * P, (b + 1) * P)
                            ps = ps_side[:, b * 2 * P:(b + 1) * 2 * P]
                            t.matmul(ps, xg_hi[:, o], hi, start=True, stop=False)
                            t.matmul(ps, xg_hi[:, o], lo, start=False, stop=False)
                            last = t.matmul(ps, xg_lo[:, o], hi, start=False, stop=True)
                        last.then_inc(s_hg, 1)
                    if s == 4 and live(i + 1):
                        pe.wait_ge(s_xn2, n + 2)
                        if gnn and live(i + 2):
                            pe.wait_ge(s_vals, n + 3)
                        elif live(i - 2):
                            pe.wait_ge(s_final, n - 1)
                        elif live(i):
                            pe.wait_ge(s_route, ROUTE * n + 1)
                        transpose4(ps_a, xn[:, 1]).then_inc(s_t2, 1)
                    if s == 5 and gnn and live(i + 2):
                        pe.wait_ge(s_edges, n + 3)
                        pe.wait_ge(s_vals_lo, n + 3)
                        for b in range(GB):
                            o = slice(b * P, (b + 1) * P)
                            t.matmul(ps_b[:, o], loop_edges[:, o], vals_hi[:, o], start=True, stop=False)
                            last = t.matmul(ps_b[:, o], loop_edges[:, o], vals_lo[:, o], start=False, stop=True)
                        last.then_inc(s_agg, 1)
                    if s == 5 and static and i == GROUPS - 1 and gnn:
                        pe.wait_ge(s_over_all, GROUPS)
                        pe.wait_ge(s_x1, GROUPS)
                        t.matmul(ps_b[0:1, 0:1], over_all[:, :], ones[:, 0:1], start=True, stop=True)\
                            .then_inc(s_over_sum, 1)

            pipeline(pe, iteration, run)

        DIRECTIONS = [
            (w_fwd, wg_fwd, b_fwd, bg_fwd, RELS // REL_CHUNK, REL_CHUNK, True, 0),
            (w_bwd, wg_bwd, b_bwd, bg_bwd, RELS // REL_CHUNK, REL_CHUNK, False, RELS // REL_CHUNK * GRAPHS),
            (w_loop, wg_loop, b_loop, bg_loop, 1, 1, False, 2 * (RELS // REL_CHUNK) * GRAPHS),
        ]
        VISITS = (2 * (RELS // REL_CHUNK) + 1) * GRAPHS

        def visits(eng, direction, visit, per_chunk=None):
            chunks, before = DIRECTIONS[direction][4], DIRECTIONS[direction][7]
            with eng.Fori(0, chunks) as chunk:
                if per_chunk is not None:
                    per_chunk(chunk)
                with eng.Fori(0, GRAPHS) as graph:
                    visit(chunk, graph, chunk * GRAPHS + graph + before)

        def chunks_before(direction):
            return DIRECTIONS[direction][7] // GRAPHS

        def general_sp(sp):
            sp.wait_ge(s_final, GROUPS)
            sp.wait_ge(s_stored, DMA * GROUPS)
            for d, (w, wg, b, bg, chunks, rels, _, before) in enumerate(DIRECTIONS):
                wait(sp, s_gen_gate_w, d)
                sp.dma_start(raw_loop[:, 0], w).then_inc(s_gen_w_loaded, DMA)
                sp.dma_start(raw_loop[:, 1], wg).then_inc(s_gen_w_loaded, DMA)

                def per_chunk(chunk, b=b, bg=bg, rels=rels, before=before):
                    wait_apart(sp, s_gen_step, (chunk * GRAPHS + before) * GEN_STEPS + 1, s_ident)
                    for n, rows in enumerate((b, bg)):
                        sp.dma_start(gen_bias[:, n, 0:rels], rows[bass.ds(chunk * rels, rels), :].partition_broadcast(P))\
                            .then_inc(s_gen_bias, DMA)

                def visit(chunk, graph, v):
                    wait_apart(sp, s_gen_in, v * 2 + 1, s_ident)
                    sp.dma_start(gen_x[:, :], x[bass.ds(graph, 1)].rearrange("g p d -> p (g d)"))\
                        .then_inc(s_gen_loaded, DMA)
                    sp.dma_start(gen_adj[:, :], adj[bass.ds(graph, 1)].rearrange("g p n -> p (g n)"))\
                        .then_inc(s_gen_loaded, DMA)

                visits(sp, d, visit, per_chunk)
            sp.wait_ge(s_gen_acc, VISITS + 1)
            with sp.Fori(0, GRAPHS) as graph:
                wait_apart(sp, s_gen_x1, graph + 1, s_ident)
                sp.dma_start(gen_x[:, :], x[bass.ds(graph, 1)].rearrange("g p d -> p (g d)"))\
                    .then_inc(s_gen_x_loaded, DMA)

        def general_pool(pool):
            pool.wait_ge(s_final, GROUPS)
            for r in range(RELS + 1):
                nc.gpsimd.memset(gen_number[:, r:r + 1], float(r + 1)).then_inc(s_gen_const, 1)

            def visit(chunk, graph, v):
                pool.wait_ge(s_gen_var, v + 1)
                nc.gpsimd.tensor_tensor(rstd[:, 0, 0:1], var_eps[:, 0, 0:1], minus_half[:, 0:1], ALU.pow)\
                    .then_inc(s_gen_rstd, 1)

            for d in range(3):
                visits(pool, d, visit)

        def general_act(act):
            act.wait_ge(s_final, GROUPS)
            for d, (_, _, _, _, _, rels, _, _) in enumerate(DIRECTIONS):
                def visit(chunk, graph, v, rels=rels):
                    act.wait_ge(s_gen_step, v * GEN_STEPS + 3)
                    nc.scalar.activation(gen_gate[:, 0:rels], gen_gate[:, 0:rels], ACT.Tanh, scale=0.5)\
                        .then_inc(s_gen_gate, 1)

                visits(act, d, visit)

        def general_pe(pe):
            t = nc.tensor
            pe.wait_ge(s_final, GROUPS)
            pe.sem_inc(s_gen_sum, 1)
            for d, (_, _, _, _, _, rels, turned, _) in enumerate(DIRECTIONS):
                pe.wait_ge(s_gen_w_loaded, DMA * 2 * (d + 1))
                pe.wait_ge(s_gen_acc, DIRECTIONS[d][7] + 1)
                for n in range(2):
                    last = t.transpose(ps_l1[0][:, n * P:(n + 1) * P], raw_loop[:, n], ident[:, :])
                last.then_inc(s_gen_w_t, 1)
                pe.wait_ge(s_gen_w, 3 * d + 2)
                t.matmul(ps_l1[1][:, 0:P], raw_loop[:, 0], wg_t[:, :], start=True, stop=True)\
                    .then_inc(s_gen_gate_w, 1)
                pe.wait_ge(s_gen_w, 3 * d + 3)

                def visit(chunk, graph, v, rels=rels, turned=turned):
                    pe.wait_ge(s_gen_in, v * 2 + 3)
                    last = t.transpose(ps_l1[0][:, 0:P], gen_xn[:, :], ident[:, :])
                    if turned:
                        last = t.transpose(ps_l1[0][:, P:2 * P], gen_rel[:, :], ident[:, :])
                    last.then_inc(s_gen_t, 1)
                    pe.wait_ge(s_gen_t_copied, v * 2 + 2)
                    t.matmul(ps_l1[1][:, 0:2 * P], gen_xn_t[:, :], gen_w[:, :, :].rearrange("p a b -> p (a b)"),
                             start=True, stop=True).then_inc(s_gen_hg, 1)
                    pe.wait_ge(s_gen_step, (v + 1) * GEN_STEPS + 1)
                    pe.wait_ge(s_gen_acc, v + 1)
                    for r in range(rels):
                        last = t.matmul(ps_l2[0][:, 0:P], gen_hot[:, r], gen_vals[:, r], start=r == 0, stop=r == rels - 1)
                    last.then_inc(s_gen_sum, 1)

                visits(pe, d, visit)

        def general_dve(dve):
            v_ = nc.vector
            dve.wait_ge(s_final, GROUPS)
            dve.wait_ge(s_stored, DMA * GROUPS)
            for counter in (s_gen_in, s_gen_step, s_gen_acc, s_gen_x1):
                dve.sem_inc(counter, 1)
            v_.memset(X[:, :], 0.0).then_inc(s_gen_const, 1)
            dve.wait_ge(s_gen_const, RELS + 2)
            for d, (_, _, _, _, _, rels, turned, _) in enumerate(DIRECTIONS):
                dve.wait_ge(s_gen_w_t, d + 1)
                wait(dve, s_gen_hg, DIRECTIONS[d][7])
                v_.tensor_copy(gen_w[:, 0], ps_l1[0][:, 0:P]).then_inc(s_gen_w, 1)
                v_.tensor_copy(wg_t[:, :], ps_l1[0][:, P:2 * P]).then_inc(s_gen_w, 1)
                dve.wait_ge(s_gen_gate_w, d + 1)
                v_.tensor_copy(gen_w[:, 1], ps_l1[1][:, 0:P]).then_inc(s_gen_w, 1)
                big = [P, rels, P]

                def visit(chunk, graph, v, rels=rels, turned=turned, big=big, d=d):
                    node = X[:, bass.ds(graph * P, P)]
                    wait_apart(dve, s_gen_loaded, (v + 1) * 2 * DMA, s_ident)
                    v_.bn_stats(stats[:, 0, 0], gen_x[:, :]).then_inc(s_gen_stats, 1)
                    wait_apart(dve, s_gen_stats, v + 1, s_ident)
                    v_.bn_aggr(mean_var[:, 0, 0], stats[:, 0, 0]).then_inc(s_gen_mean, 1)
                    dve.wait_ge(s_gen_mean, v + 1)
                    v_.tensor_scalar(var_eps[:, 0, 0:1], mean_var[:, 0, 0, 1:2], LN_EPS, None, ALU.add)\
                        .then_inc(s_gen_var, 1)
                    dve.wait_ge(s_gen_rstd, v + 1)
                    v_.tensor_scalar(gen_xn[:, :], gen_x[:, :], mean_var[:, 0, 0, 0:1], rstd[:, 0, 0:1],
                                     ALU.subtract, ALU.mult).then_inc(s_gen_in, 1)
                    dve.wait_ge(s_gen_step, v * GEN_STEPS + 1)
                    v_.tensor_copy(gen_rel[:, :], gen_adj[:, :]).then_inc(s_gen_in, 1)
                    dve.wait_ge(s_gen_t, v + 1)
                    v_.tensor_copy(gen_xn_t[:, :], ps_l1[0][:, 0:P]).then_inc(s_gen_t_copied, 1)
                    rel = gen_rel_t if turned else gen_rel
                    if turned:
                        v_.tensor_copy(gen_rel_t[:, :], ps_l1[0][:, P:2 * P]).then_inc(s_gen_t_copied, 1)
                    else:
                        v_.tensor_copy(gen_rel_t[:, :], gen_rel[:, :]).then_inc(s_gen_t_copied, 1)
                    dve.wait_ge(s_gen_hg, v + 1)
                    v_.tensor_copy(gen_hg[:, :, :], ps_l1[1][:, 0:2 * P].rearrange("p (a b) -> p a b", a=2))\
                        .then_inc(s_gen_step, 1)
                    dve.wait_ge(s_gen_step, v * GEN_STEPS + 2)
                    dve.wait_ge(s_gen_bias, (chunk + chunks_before(d) + 1) * 2 * DMA)
                    v_.tensor_tensor(gen_gate[:, 0:rels], gen_bias[:, 1, 0:rels],
                                     gen_hg[:, 1].unsqueeze(1).to_broadcast(big), ALU.add).then_inc(s_gen_step, 1)
                    dve.wait_ge(s_gen_sum, v + 1)
                    v_.tensor_tensor(gen_vals[:, 0:rels], gen_bias[:, 0, 0:rels],
                                     gen_hg[:, 0].unsqueeze(1).to_broadcast(big), ALU.add).then_inc(s_gen_step, 1)
                    numbers = gen_number[:, 0:1] if d == 2 else gen_number[:, bass.ds(chunk * rels + 1, rels)]
                    dve.wait_ge(s_gen_t_copied, v * 2 + 2)
                    v_.tensor_tensor(gen_hot[:, 0:rels], rel[:, :].unsqueeze(1).to_broadcast(big),
                                     numbers.unsqueeze(2).to_broadcast(big), ALU.is_equal).then_inc(s_gen_step, 1)
                    dve.wait_ge(s_gen_gate, v + 1)
                    dve.wait_ge(s_gen_step, v * GEN_STEPS + 5)
                    v_.scalar_tensor_tensor(gen_vals[:, 0:rels], gen_gate[:, 0:rels], 1.0, gen_vals[:, 0:rels],
                                            ALU.add, ALU.mult).then_inc(s_gen_step, 1)
                    dve.wait_ge(s_gen_sum, v + 2)
                    dve.wait_ge(s_gen_acc, v + 1)
                    v_.scalar_tensor_tensor(node, ps_l2[0][:, 0:P], 0.5, node, ALU.mult, ALU.add)\
                        .then_inc(s_gen_acc, 1)

                visits(dve, d, visit)
            dve.wait_ge(s_gen_acc, VISITS + 1)
            with dve.Fori(0, GRAPHS) as graph:
                node = X[:, bass.ds(graph * P, P)]
                dve.wait_ge(s_gen_x_loaded, (graph + 1) * DMA)
                v_.scalar_tensor_tensor(node, node, 0.0, gen_x[:, :], ALU.max, ALU.add).then_inc(s_gen_x1, 1)
            dve.wait_ge(s_gen_x1, GRAPHS + 1)

        def if_general(eng, general, again):
            eng.wait_ge(s_flag, 1)
            found = eng.value_load(flag[0:1, 0:1], min_val=0, max_val=1)
            with eng.If_ne(eng.to_reg(found), 0):
                general(eng)
                again(eng, 1)

        with nc.Block() as block:
            @block.sync
            def _(sp):
                sp_pipeline(sp, 0)
                if_general(sp, general_sp, sp_pipeline)

            @block.gpsimd
            def _(pool):
                pool_constants(pool)
                pool_pipeline(pool, 0)
                if_general(pool, general_pool, pool_pipeline)

            @block.scalar
            def _(act):
                act_pipeline(act, 0)
                if_general(act, general_act, act_pipeline)

            @block.vector
            def _(dve):
                prepare_hg(dve)
                dve_pipeline(dve, 0)
                if_general(dve, general_dve, dve_pipeline)

            @block.tensor
            def _(pe):
                pe_setup(pe)
                pe_pipeline(pe, 0)
                if_general(pe, general_pe, pe_pipeline)


_INS = ['x', 'adj'] + ['L0_gnn_' + n for n in (
    'W_fwd', 'W_bwd', 'W_loop', 'Wg_fwd', 'Wg_bwd', 'Wg_loop', 'b_fwd', 'b_bwd', 'b_loop', 'bg_fwd', 'bg_bwd',
    'bg_loop')] + ['L0_ffn_' + n for n in (
        'router_w1', 'router_b1', 'router_w2', 'router_b2', 'expert_w1', 'expert_b1', 'expert_w2', 'expert_b2',
        'expert_w3', 'expert_b3')]


def kernel(**inputs):
    import numpy as _np
    import concourse.bacc as _bacc
    from concourse.bass_utils import run_bass_kernel_spmd as _run

    nc = _bacc.Bacc("TRN2", target_bir_lowering=False, num_devices=1)
    arrays, args = {}, []
    for name in _INS:
        a = _np.ascontiguousarray(inputs[name])
        arrays[f"in_{name}_dram"] = a
        args.append(nc.dram_tensor(f"in_{name}_dram", a.shape, mybir.dt.from_np(a.dtype), kind="ExternalInput").ap())
    out = nc.dram_tensor("out_0_dram", (GRAPHS, P, P), F32, kind="ExternalOutput").ap()
    adj_ffn_kernel(nc, *args, out)
    r = _run(nc, [arrays], core_ids=[0])
    return r.results[0]["out_0_dram"]
```

```python
from contextlib import ExitStack

import concourse.bass as bass
from concourse import mybir

F32 = mybir.dt.float32
F32R = mybir.dt.float32r
I32 = mybir.dt.int32
ALU = mybir.AluOpType
ACT = mybir.ActivationFunctionType
AX = mybir.AxisListType

P = 128
GRAPHS = 64
GB = 4
TOK = GB * P
GROUPS = GRAPHS // GB
EXPERTS = 6
ROUTER_H = 64
RELS = 39
REL_CHUNK = 13
R1_RING = EXPERTS
R2_RING = 3
LN_EPS = 1e-5
BLK = 32
DMA = 16


def wait(eng, sem, value):
    if not (isinstance(value, int) and value <= 0):
        eng.wait_ge(sem, value)


def wait_apart(eng, sem, value, reached):
    if not isinstance(value, int):
        value = eng.snap(eng.to_reg(value))
    eng.wait_ge(reached, 1)
    wait(eng, sem, value)


def live(g):
    return not isinstance(g, int) or 0 <= g < GROUPS


def pipeline(eng, iteration, run=0, ahead=3):
    last = (GROUPS - ahead) // 2
    for i in range(-3, 2):
        iteration(i, i + GROUPS * run, i % 2)
    with eng.Fori(1, last) as pair:
        for parity in range(2):
            i = pair * 2 + parity
            iteration(i, i + GROUPS * run, parity)
    for i in range(2 * last, GROUPS + 2):
        iteration(i, i + GROUPS * run, i % 2)


def adj_ffn_kernel(nc, x, adj, w_fwd, w_bwd, w_loop, wg_fwd, wg_bwd, wg_loop, b_fwd, b_bwd, b_loop,
                   bg_fwd, bg_bwd, bg_loop, router_w1, router_b1, router_w2, router_b2,
                   expert_w1, expert_b1, expert_w2, expert_b2, expert_w3, expert_b3, out):
    with ExitStack() as ctx:
        ctx.enter_context(nc.allow_non_contiguous_dma(reason="bias columns and rows of tokens"))

        def sb(name, shape, dt=F32):
            return ctx.enter_context(nc.sbuf_tensor(name, shape, dt))

        def sem(name):
            return ctx.enter_context(nc.semaphore(name))

        ident = sb("ident", [P, P])
        raw_w = [sb(f"raw_w{n}", [P, EXPERTS, P]) for n in range(3)]
        w_hi = [sb(f"w_hi{n}", [P, EXPERTS, P], F32R) for n in range(3)]
        w_lo = [sb(f"w_lo{n}", [P, EXPERTS, P], F32R) for n in range(3)]
        bias2 = sb("bias2", [P, EXPERTS])
        raw_b3 = sb("raw_b3", [P, P])
        b3_split = sb("b3_split", [P, P], F32R)
        select = sb("select", [P, EXPERTS, P], F32R)
        raw_b1 = sb("raw_b1", [P, EXPERTS, P])
        raw_router = sb("raw_router", [P, P])
        raw_router_b = sb("raw_router_b", [P, P])
        router_hi = sb("router_hi", [P, P], F32R)
        router_lo = sb("router_lo", [P, P], F32R)
        logit_w = sb("logit_w", [P, EXPERTS])
        logit_bias = sb("logit_bias", [P, EXPERTS])
        priority = sb("priority", [P, GB, EXPERTS])
        minus_half = sb("minus_half", [P, GB])
        raw_loop = sb("raw_loop", [P, 2, P])
        wg_t = sb("wg_t", [P, P])
        hg = sb("hg", [P, 2, P])
        hg_hi = sb("hg_hi", [P, 2, P], F32R)
        hg_lo = sb("hg_lo", [P, 2, P], F32R)
        raw_hg_b = sb("raw_hg_b", [P, 2, P])
        ones = sb("ones", [P, P])

        X = sb("X", [P, GROUPS * TOK])
        adj_in = sb("adj_in", [P, 2, TOK], I32)
        loop_edges = sb("loop_edges", [P, TOK], F32R)
        over_one = sb("over_one", [P, TOK])
        over_sum = sb("over_sum", [P, 2])
        over_all = sb("over_all", [P, 1])
        minus_one = sb("minus_one", [P, 1])
        stats = sb("stats", [P, 2, GB, 6])
        mean_var = sb("mean_var", [P, 2, GB, 2])
        var_eps = sb("var_eps", [P, 2, GB])
        rstd = sb("rstd", [P, 2, GB])
        spread = sb("spread", [P, 2, GB])
        centre = sb("centre", [P, 2, GB])
        xn = sb("xn", [P, 2, TOK])
        xg_hi = sb("xg_hi", [P, TOK], F32R)
        xg_lo = sb("xg_lo", [P, TOK], F32R)
        gate = sb("gate", [P, GB, P])
        vals = sb("vals", [P, GB, P])
        vals_hi = sb("vals_hi", [P, TOK], F32R)
        vals_lo = sb("vals_lo", [P, TOK], F32R)
        xf_hi = sb("xf_hi", [P, 2, TOK], F32R)
        xf_lo = sb("xf_lo", [P, 2, TOK], F32R)
        router_h = sb("router_h", [P, TOK])
        rt = {n: sb("rt_" + n, [P, GB, EXPERTS]) for n in
              ("z", "shifted", "exp", "p", "rest", "hit", "rank", "first", "second", "both", "diff", "tilt", "w")}
        rc = {n: sb("rc_" + n, [P, GB]) for n in
              ("max", "sum", "rsum", "p1", "p2", "best1", "best2", "gap", "tanh")}
        w_parts = sb("w_parts", [P, GB, P])
        w_blocks_f = w_parts[:, :, :].rearrange("p b (q c) -> p b q c", c=BLK)
        w_blocks = w_parts[:, :, :].bitcast(F32R).rearrange("p b (q c) -> p b q c", c=BLK)
        w_rows = sb("w_rows", [P, TOK], F32R)
        r1_hi = sb("r1_hi", [P, R1_RING, TOK], F32R)
        r1_lo = sb("r1_lo", [P, R1_RING, TOK], F32R)
        u2 = sb("u2", [P, 2, TOK])
        v2 = sb("v2", [P, 2, TOK])
        r2_hi = sb("r2_hi", [P, R2_RING, TOK], F32R)
        r2_lo = sb("r2_lo", [P, R2_RING, TOK], F32R)
        ffn_t = sb("ffn_t", [P, TOK])

        flag = sb("flag", [1, 1], I32)
        gen_x = sb("gen_x", [P, P])
        gen_adj = sb("gen_adj", [P, P], I32)
        gen_xn = sb("gen_xn", [P, P])
        gen_xn_t = sb("gen_xn_t", [P, P])
        gen_rel = sb("gen_rel", [P, P])
        gen_rel_t = sb("gen_rel_t", [P, P])
        gen_hg = sb("gen_hg", [P, 2, P])
        gen_w = sb("gen_w", [P, 2, P])
        gen_bias = sb("gen_bias", [P, 2, REL_CHUNK, P])
        gen_vals = sb("gen_vals", [P, REL_CHUNK, P])
        gen_gate = sb("gen_gate", [P, REL_CHUNK, P])
        gen_hot = sb("gen_hot", [P, REL_CHUNK, P])
        gen_number = sb("gen_number", [P, RELS + 1])

        ps_l1 = [ctx.enter_context(nc.psum_tensor(f"ps_l1_{n}", [P, TOK], F32)) for n in range(2)]
        ps_l2 = [ctx.enter_context(nc.psum_tensor(f"ps_l2_{n}", [P, TOK], F32)) for n in range(2)]
        ps_l3 = ctx.enter_context(nc.psum_tensor("ps_l3", [P, TOK], F32))
        ps_w = ctx.enter_context(nc.psum_tensor("ps_w", [P, TOK], F32))
        ps_side = ctx.enter_context(nc.psum_tensor("ps_side", [P, 2 * TOK], F32))
        ps_a, ps_b = ps_side[:, 0:TOK], ps_side[:, TOK:2 * TOK]
        ps_hg = ps_side[:, :].rearrange("p (b c) -> p b c", c=2 * P)

        s_w1_loaded = sem("s_w1_loaded")
        s_rest_loaded = sem("s_rest_loaded")
        s_hg_loaded = sem("s_hg_loaded")
        s_zeroed = sem("s_zeroed")
        s_ident = sem("s_ident")
        s_loop_t = sem("s_loop_t")
        s_gate_w = sem("s_gate_w")
        s_col_sums = sem("s_col_sums")
        s_prep_hg = sem("s_prep_hg")
        s_prep = sem("s_prep")
        s_w1_hi = sem("s_w1_hi")
        s_w1_lo = sem("s_w1_lo")
        s_rest_hi = sem("s_rest_hi")
        s_rest_lo = sem("s_rest_lo")
        s_const = sem("s_const")
        s_x_loaded = [sem(f"s_x_loaded{n}") for n in range(2)]
        s_adj_loaded = [sem(f"s_adj_loaded{n}") for n in range(2)]
        s_stored = sem("s_stored")
        s_stats = [sem(f"s_stats{n}") for n in range(2)]
        s_mean_var = [sem(f"s_mean_var{n}") for n in range(2)]
        s_ln1 = sem("s_ln1")
        s_rstd1 = sem("s_rstd1")
        s_xn1 = sem("s_xn1")
        s_t1 = sem("s_t1")
        s_xg_hi = sem("s_xg_hi")
        s_xg_lo = sem("s_xg_lo")
        s_hg = sem("s_hg")
        s_gate = sem("s_gate")
        s_vals = sem("s_vals")
        s_vals_hi = sem("s_vals_hi")
        s_vals_lo = sem("s_vals_lo")
        s_edges = sem("s_edges")
        s_over = sem("s_over")
        s_over_all = sem("s_over_all")
        s_agg = sem("s_agg")
        s_x1 = sem("s_x1")
        s_ln2 = sem("s_ln2")
        s_rstd2 = sem("s_rstd2")
        s_xn2 = sem("s_xn2")
        s_t2 = sem("s_t2")
        s_xf_hi = sem("s_xf_hi")
        s_xf_lo = sem("s_xf_lo")
        s_rh = sem("s_rh")
        s_router_h = sem("s_router_h")
        s_logits = sem("s_logits")
        s_route = sem("s_route")
        s_route_act = sem("s_route_act")
        s_w_t = sem("s_w_t")
        s_w_rows = sem("s_w_rows")
        s_l1 = sem("s_l1")
        s_r1_hi = sem("s_r1_hi")
        s_r1_lo = sem("s_r1_lo")
        s_l2 = sem("s_l2")
        s_wb = sem("s_wb")
        s_u2 = sem("s_u2")
        s_v2 = sem("s_v2")
        s_r2_hi = sem("s_r2_hi")
        s_r2_lo = sem("s_r2_lo")
        s_l3 = sem("s_l3")
        s_ffn_t = sem("s_ffn_t")
        s_out_t = sem("s_out_t")
        s_final = sem("s_final")
        s_over_sum = sem("s_over_sum")
        s_flag = sem("s_flag")
        s_gen_w_loaded = sem("s_gen_w_loaded")
        s_gen_w_t = sem("s_gen_w_t")
        s_gen_w = sem("s_gen_w")
        s_gen_gate_w = sem("s_gen_gate_w")
        s_gen_bias = sem("s_gen_bias")
        s_gen_const = sem("s_gen_const")
        s_gen_loaded = sem("s_gen_loaded")
        s_gen_stats = sem("s_gen_stats")
        s_gen_mean = sem("s_gen_mean")
        s_gen_var = sem("s_gen_var")
        s_gen_rstd = sem("s_gen_rstd")
        s_gen_in = sem("s_gen_in")
        s_gen_t = sem("s_gen_t")
        s_gen_t_copied = sem("s_gen_t_copied")
        s_gen_hg = sem("s_gen_hg")
        s_gen_step = sem("s_gen_step")
        s_gen_gate = sem("s_gen_gate")
        s_gen_sum = sem("s_gen_sum")
        s_gen_acc = sem("s_gen_acc")
        s_gen_x_loaded = sem("s_gen_x_loaded")
        s_gen_x1 = sem("s_gen_x1")
        GEN_STEPS = 5
        ROUTE = 24

        x_v = x.rearrange("(g b) p d -> p g b d", b=GB)
        adj_v = adj.rearrange("(g b) p n -> p g b n", b=GB)
        out_v = out.rearrange("(g b) p d -> p g b d", b=GB)

        def X_of(g, b=None):
            if b is None:
                return X[:, bass.ds(g * TOK, TOK)]
            return X[:, bass.ds(g * TOK + b * P, P)]

        def tok3(ap):
            return ap.rearrange("p (b d) -> p b d", b=GB)

        N_HG, N_W1, N_REST = 4, 6, 9
        N_PREP_HG = 7
        N_PREP, N_REST_HI, N_REST_LO = 6, 3, 4
        N_CONST = 3 + EXPERTS + 2

        def loads(g):
            return DMA * (g // 2 + 1)


        def load_first(act):
            act.dma_start(raw_loop[:, 0], w_loop).then_inc(s_hg_loaded, DMA)
            act.dma_start(raw_loop[:, 1], wg_loop).then_inc(s_hg_loaded, DMA)
            act.dma_start(raw_hg_b[:, 0], b_loop[0].partition_broadcast(P)).then_inc(s_hg_loaded, DMA)
            act.dma_start(raw_hg_b[:, 1], bg_loop[0].partition_broadcast(P)).then_inc(s_hg_loaded, DMA)
            act.dma_start(raw_w[0][:, :, :], expert_w1.rearrange("e d f -> d e f")).then_inc(s_w1_loaded, DMA)
            act.dma_start(raw_b1[:, :, :], expert_b1.partition_broadcast(P)).then_inc(s_w1_loaded, DMA)
            for half in range(2):
                o = slice(half * ROUTER_H, (half + 1) * ROUTER_H)
                act.dma_start(raw_router[:, o], router_w1).then_inc(s_w1_loaded, DMA)
                act.dma_start(raw_router_b[:, o], router_b1.partition_broadcast(P)).then_inc(s_w1_loaded, DMA)

        def load_rest(sp):
            for n, w in ((1, expert_w2), (2, expert_w3)):
                sp.dma_start(raw_w[n][:, :, :], w.rearrange("e d f -> d e f")).then_inc(s_rest_loaded, DMA)
            sp.dma_start(logit_bias[:, :], router_b2.partition_broadcast(P)).then_inc(s_rest_loaded, DMA)
            sp.dma_start(bias2[:, :], expert_b2.rearrange("e h -> h e")).then_inc(s_rest_loaded, DMA)
            sp.wait_ge(s_zeroed, 2)
            sp.dma_start(logit_w[0:ROUTER_H], router_w2).then_inc(s_rest_loaded, DMA)
            for n in range(4):
                sp.dma_start(raw_b3[n * BLK:n * BLK + EXPERTS], expert_b3).then_inc(s_rest_loaded, DMA)

        def sp_pipeline(sp, run):
            def load(g, parity):
                wait_apart(sp, s_ln1, g - 1, s_ident)
                wait(sp, s_edges, g - 1)
                wait(sp, s_over, g - 1)
                sp.dma_start(tok3(X_of(g)), x_v[:, bass.ds(g, 1)].rearrange("p g b d -> p (g b) d"))\
                    .then_inc(s_x_loaded[parity], DMA)
                sp.dma_start(tok3(adj_in[:, parity]), adj_v[:, bass.ds(g, 1)].rearrange("p g b d -> p (g b) d"))\
                    .then_inc(s_adj_loaded[parity], DMA)

            def iteration(i, n, parity):
                if run == 0 and isinstance(i, int) and i == -2:
                    load_rest(sp)
                if run == 0 and live(i + 4):
                    load(i + 4, parity)
                if live(i - 2):
                    wait_apart(sp, s_final, n - 1, s_ident)
                    sp.dma_start(out_v[:, bass.ds(i - 2, 1)].rearrange("p g b d -> p (g b) d"), tok3(X_of(i - 2)))\
                        .then_inc(s_stored, DMA)

            if run == 0:
                sp.wait_ge(s_ident, 1)
                load(0, 0)
            pipeline(sp, iteration, run, ahead=4)
            sp.wait_ge(s_stored, DMA * GROUPS * (run + 1))

        def pool_constants(pool):
            nc.gpsimd.memset(ident[:, :], 0.0).then_inc(s_ident, 1)
            nc.gpsimd.memset(logit_w[:, :], 0.0).then_inc(s_zeroed, 1)
            nc.gpsimd.memset(raw_b3[:, :], 0.0).then_inc(s_zeroed, 1)
            pool.wait_ge(s_ident, 1)
            nc.gpsimd.affine_select(out=ident[:, :], in_=ident[:, :], compare_op=ALU.not_equal, fill=1.0,
                                    base=0, pattern=[[-1, P]], channel_multiplier=1).then_inc(s_ident, 1)
            nc.gpsimd.memset(minus_half[:, :], -0.5).then_inc(s_const, 1)
            nc.gpsimd.memset(ones[:, :], 1.0).then_inc(s_const, 1)
            nc.gpsimd.memset(w_parts[:, :, :], 0.0).then_inc(s_const, 1)
            for e in range(EXPERTS):
                nc.gpsimd.memset(priority[:, :, e:e + 1], float(EXPERTS - e)).then_inc(s_const, 1)
            nc.gpsimd.memset(minus_one[:, :], -1.0).then_inc(s_const, 1)
            nc.gpsimd.memset(over_all[:, :], 0.0).then_inc(s_const, 1)
            pool.wait_ge(s_const, 1)

        def pool_pipeline(pool, run):
            gnn = run == 0

            def low(tile, raw, high, done):
                nc.gpsimd.tensor_tensor(tile, raw, high.bitcast(F32), ALU.subtract).then_inc(done, 1)

            def second_weights_low():
                pool.wait_ge(s_rest_hi, 1)
                low(w_lo[1][:, :, :], raw_w[1][:, :, :], w_hi[1][:, :, :], s_rest_lo)

            def first_weights_low():
                pool.wait_ge(s_w1_hi, 1)
                low(w_lo[0][:, :, :], raw_w[0][:, :, :], w_hi[0][:, :, :], s_w1_lo)

            def rest_low():
                pool.wait_ge(s_rest_hi, N_REST_HI)
                low(w_lo[2][:, :, :], raw_w[2][:, :, :], w_hi[2][:, :, :], s_rest_lo)
                pool.wait_ge(s_rest_lo, 2)
                low(b3_split[2 * BLK:], raw_b3[2 * BLK:], b3_split[2 * BLK:], s_rest_lo)
                pool.wait_ge(s_rest_lo, 3)
                nc.gpsimd.tensor_tensor(select[:, :, :],
                                        ident[:, 0:EXPERTS].unsqueeze(2).to_broadcast([P, EXPERTS, P]),
                                        ident[:, BLK:BLK + EXPERTS].unsqueeze(2).to_broadcast([P, EXPERTS, P]),
                                        ALU.add).then_inc(s_rest_lo, 1)

            def scale(norm, c, s_var, s_rstd, s_xn):
                pool.wait_ge(s_var, c + 1)
                wait(pool, s_xn, c)
                nc.gpsimd.tensor_tensor(rstd[:, norm], var_eps[:, norm], minus_half[:, :], ALU.pow)\
                    .then_inc(s_rstd, 1)
                pool.wait_ge(s_rstd, 3 * c + 1)
                nc.gpsimd.tensor_tensor(spread[:, norm], var_eps[:, norm], rstd[:, norm], ALU.mult)\
                    .then_inc(s_rstd, 1)
                pool.wait_ge(s_rstd, 3 * c + 2)
                nc.gpsimd.tensor_tensor(centre[:, norm], mean_var[:, norm, :, 0], spread[:, norm], ALU.subtract)\
                    .then_inc(s_rstd, 1)

            def iteration(i, n, parity):
                def set_up(at, prepare):
                    if run == 0 and isinstance(i, int) and i == at:
                        prepare()

                def scale1(d):
                    if gnn and live(i + d):
                        scale(0, n + d, s_ln1, s_rstd1, s_xn1)

                def scale2(d):
                    if live(i + d):
                        scale(1, n + d, s_ln2, s_rstd2, s_xn2)

                def values_low(d):
                    if gnn and live(i + d):
                        c = n + d
                        pool.wait_ge(s_vals_hi, c + 1)
                        wait(pool, s_agg, c)
                        nc.gpsimd.tensor_tensor(tok3(vals_lo[:, :]), vals[:, :, :], tok3(vals_hi[:, :]).bitcast(F32),
                                                ALU.subtract).then_inc(s_vals_lo, 1)

                def weighted_low(d, e):
                    if live(i + d):
                        k = EXPERTS * (n + d) + e
                        pool.wait_ge(s_r2_hi, k + 1)
                        wait(pool, s_l3, k + 1 - R2_RING)
                        nc.gpsimd.tensor_tensor(r2_lo[:, e % R2_RING], v2[:, e % 2], r2_hi[:, e % R2_RING].bitcast(F32),
                                                ALU.subtract).then_inc(s_r2_lo, 1)

                weighted_low(-1, 1)
                weighted_low(-1, 2)
                weighted_low(-1, 3)
                scale1(3)
                values_low(2)
                set_up(-2, second_weights_low)
                set_up(-2, first_weights_low)
                set_up(-1, rest_low)
                weighted_low(-1, 4)
                weighted_low(-1, 5)
                weighted_low(0, 0)
                scale2(2)

            pipeline(pool, iteration, run)

        def act_pipeline(act, run):
            gnn = run == 0

            def first_weights_high():
                act.wait_ge(s_prep, N_PREP)
                nc.scalar.activation(w_hi[0][:, :, :], raw_w[0][:, :, :], ACT.Copy).then_inc(s_w1_hi, 1)

            def rest_high():
                act.wait_ge(s_rest_loaded, DMA * N_REST)
                for tile, raw in ((w_hi[1], raw_w[1]), (w_hi[2], raw_w[2])):
                    nc.scalar.activation(tile[:, :, :], raw[:, :, :], ACT.Copy).then_inc(s_rest_hi, 1)
                nc.scalar.activation(b3_split[:, :], raw_b3[:, :], ACT.Copy).then_inc(s_rest_hi, 1)

            def iteration(i, n, parity):
                def set_up(at, prepare):
                    if run == 0 and isinstance(i, int) and i == at:
                        prepare()

                def norm1_high(d):
                    if gnn and live(i + d):
                        c = n + d
                        act.wait_ge(s_t1, c + 1)
                        wait(act, s_hg, c)
                        nc.scalar.activation(xg_hi[:, :], ps_b, ACT.Copy).then_inc(s_xg_hi, 1)

                def gate_tanh(d):
                    if gnn and live(i + d):
                        c = n + d
                        act.wait_ge(s_hg, c + 1)
                        wait(act, s_vals, c)
                        nc.scalar.activation(gate[:, :, :], ps_hg[:, :, P:2 * P], ACT.Tanh, scale=0.5)\
                            .then_inc(s_gate, 1)

                def values_high(d):
                    if gnn and live(i + d):
                        c = n + d
                        act.wait_ge(s_vals, c + 1)
                        wait(act, s_agg, c)
                        nc.scalar.activation(tok3(vals_hi[:, :]), vals[:, :, :], ACT.Copy).then_inc(s_vals_hi, 1)

                def sum_over(d):
                    if gnn and live(i + d):
                        c, buf = n + d, (parity + d) % 2
                        act.wait_ge(s_adj_loaded[buf], loads(i + d))
                        wait(act, s_over, c)
                        wait(act, s_over_all, c - 1)
                        nc.scalar.activation(over_one[:, :], adj_in[:, buf], ACT.Relu, bias=minus_one[:, :],
                                             accum_out=over_sum[:, buf:buf + 1]).then_inc(s_over, 1)

                def norm2_high(d):
                    if live(i + d):
                        c = n + d
                        act.wait_ge(s_t2, c + 1)
                        wait(act, s_l1, EXPERTS * (c - 1))
                        nc.scalar.activation(xf_hi[:, (parity + d) % 2], ps_a, ACT.Copy).then_inc(s_xf_hi, 1)

                def router_relu(d):
                    if live(i + d):
                        c = n + d
                        act.wait_ge(s_rh, c + 1)
                        wait(act, s_logits, c)
                        nc.scalar.activation(router_h[:, :], ps_a, ACT.Relu).then_inc(s_router_h, 1)

                def exponentials(d):
                    if live(i + d):
                        act.wait_ge(s_route, ROUTE * (n + d) + 3)
                        nc.scalar.activation(rt["exp"][:, :, :], rt["shifted"][:, :, :], ACT.Exp)\
                            .then_inc(s_route_act, 1)

                def gap_tanh(d):
                    if live(i + d):
                        act.wait_ge(s_route, ROUTE * (n + d) + 18)
                        nc.scalar.activation(rc["tanh"][:, :], rc["gap"][:, :], ACT.Tanh, scale=0.5)\
                            .then_inc(s_route_act, 1)

                def copy_weights(d):
                    if live(i + d):
                        act.wait_ge(s_w_t, n + d + 1)
                        nc.scalar.activation(w_rows[:, :], ps_w[:, :], ACT.Copy).then_inc(s_w_rows, 1)

                def first_relu(d, e):
                    if live(i + d):
                        k = EXPERTS * (n + d) + e
                        act.wait_ge(s_l1, k + 1)
                        wait(act, s_l2, k + 1 - R1_RING)
                        nc.scalar.activation(r1_hi[:, e], ps_l1[e % 2][:, :], ACT.Relu).then_inc(s_r1_hi, 1)

                def second_relu(d, e):
                    if live(i + d):
                        k = EXPERTS * (n + d) + e
                        if run == 0 and isinstance(k, int) and k == 0:
                            act.wait_ge(s_rest_loaded, DMA * N_REST)
                        act.wait_ge(s_l2, k + 1)
                        wait(act, s_v2, k - 1)
                        nc.scalar.activation(u2[:, e % 2], ps_l2[e % 2][:, :], ACT.Relu, bias=bias2[:, e:e + 1])\
                            .then_inc(s_u2, 1)

                def weighted_high(d, e):
                    if live(i + d):
                        k = EXPERTS * (n + d) + e
                        act.wait_ge(s_v2, k + 1)
                        wait(act, s_l3, k + 1 - R2_RING)
                        nc.scalar.activation(r2_hi[:, e % R2_RING], v2[:, e % 2], ACT.Copy).then_inc(s_r2_hi, 1)

                def copy_output(d):
                    if live(i + d):
                        act.wait_ge(s_l3, EXPERTS * (n + d + 1))
                        nc.scalar.activation(ffn_t[:, :], ps_l3[:, :], ACT.Copy).then_inc(s_ffn_t, 1)

                first_relu(-1, 3)
                first_relu(-1, 4)
                router_relu(0)
                copy_weights(-1)
                second_relu(-1, 1)
                norm1_high(2)
                first_relu(-1, 5)
                weighted_high(-1, 0)
                second_relu(-1, 2)
                exponentials(0)
                copy_output(-2)
                weighted_high(-1, 1)
                first_relu(0, 0)
                second_relu(-1, 3)
                sum_over(2)
                weighted_high(-1, 2)
                second_relu(-1, 4)
                first_relu(0, 1)
                gate_tanh(2)
                weighted_high(-1, 3)
                first_relu(0, 2)
                set_up(-2, rest_high)
                second_relu(-1, 5)
                values_high(2)
                norm2_high(1)
                set_up(-2, first_weights_high)
                second_relu(0, 0)
                weighted_high(-1, 4)
                gap_tanh(0)
                weighted_high(-1, 5)

            if run == 0:
                load_first(act)
                act.wait_ge(s_const, N_CONST)
            pipeline(act, iteration, run)

        def shift_and_split(dve, w, bias, ps, w_hi_, w_lo_, counter, done):
            nc.vector.tensor_tensor(bias, bias, ps, ALU.subtract).then_inc(counter, 1)
            dve.wait_ge(counter, done + 1)
            nc.vector.scalar_tensor_tensor(w, bias, 1.0 / P, w, ALU.mult, ALU.add).then_inc(counter, 1)
            dve.wait_ge(counter, done + 2)
            nc.vector.tensor_copy(w_hi_, w).then_inc(counter, 1)
            dve.wait_ge(counter, done + 3)
            nc.vector.tensor_tensor(w_lo_, w, w_hi_.bitcast(F32), ALU.subtract).then_inc(counter, 1)

        def prepare_hg(dve):
            v = nc.vector
            dve.wait_ge(s_hg_loaded, DMA * N_HG)
            dve.wait_ge(s_loop_t, 2)
            v.tensor_copy(wg_t[:, :], ps_l1[0][:, P:2 * P]).then_inc(s_prep_hg, 1)
            v.tensor_scalar(hg[:, 0], ps_l1[0][:, 0:P], 0.5, None, ALU.mult)
            v.tensor_scalar(raw_hg_b[:, 0], raw_hg_b[:, 0], 0.5, None, ALU.mult)
            dve.wait_ge(s_gate_w, 1)
            v.tensor_copy(hg[:, 1], ps_l1[1][:, 0:P]).then_inc(s_prep_hg, 2)

        def prepare_hg_parts(dve):
            dve.wait_ge(s_col_sums, 1)
            shift_and_split(dve, hg[:, :, :], raw_hg_b[:, :, :],
                            ps_l2[0][:, 0:2 * P].rearrange("p (a b) -> p a b", a=2),
                            hg_hi[:, :, :], hg_lo[:, :, :], s_prep_hg, 3)

        def prepare_first(dve):
            dve.wait_ge(s_w1_loaded, DMA * N_W1)
            dve.wait_ge(s_col_sums, 2)
            shift_and_split(dve, raw_router[:, :], raw_router_b[:, :], ps_w[:, 0:P], router_hi[:, :],
                            router_lo[:, :], s_prep, 0)
            half = EXPERTS // 2
            dve.wait_ge(s_col_sums, 3)
            for n in range(2):
                e = slice(n * half, (n + 1) * half)
                last = nc.vector.tensor_tensor(raw_b1[:, e], raw_b1[:, e],
                                               ps_l2[n][:, 0:half * P].rearrange("p (e f) -> p e f", e=half),
                                               ALU.subtract)
            last.then_inc(s_prep, 1)
            dve.wait_ge(s_prep, 5)
            nc.vector.scalar_tensor_tensor(raw_w[0][:, :, :], raw_b1[:, :, :], 1.0 / P, raw_w[0][:, :, :],
                                           ALU.mult, ALU.add).then_inc(s_prep, 1)
            dve.wait_ge(s_rest_loaded, DMA * N_REST)
            dve.wait_ge(s_const, N_CONST)

        def dve_pipeline(dve, run):
            v = nc.vector
            gnn = run == 0

            def route_steps(c, first, last):
                wide = [P, GB, EXPERTS]

                def bc(tile):
                    return tile[:, :].unsqueeze(2).to_broadcast(wide)

                R = {name: t[:, :, :] for name, t in rt.items()}
                steps = {
                    1: lambda: v.tensor_tensor(R["z"], ps_a[:, 0:GB * EXPERTS].rearrange("p (b e) -> p b e", b=GB),
                                               logit_bias[:, :].unsqueeze(1).to_broadcast(wide), ALU.add),
                    2: lambda: v.tensor_reduce(rc["max"][:, :], R["z"], AX.X, ALU.max),
                    3: lambda: v.tensor_tensor(R["shifted"], R["z"], bc(rc["max"]), ALU.subtract),
                    4: lambda: v.tensor_reduce(rc["sum"][:, :], R["exp"], AX.X, ALU.add),
                    5: lambda: v.reciprocal(rc["rsum"][:, :], rc["sum"][:, :]),
                    6: lambda: v.tensor_tensor(R["p"], R["exp"], bc(rc["rsum"]), ALU.mult),
                    7: lambda: v.tensor_reduce(rc["p1"][:, :], R["p"], AX.X, ALU.max),
                    8: lambda: v.tensor_tensor(R["hit"], R["p"], bc(rc["p1"]), ALU.is_equal),
                    9: lambda: v.tensor_tensor(R["rank"], R["hit"], priority[:, :, :], ALU.mult),
                    10: lambda: v.tensor_reduce(rc["best1"][:, :], R["rank"], AX.X, ALU.max),
                    11: lambda: v.tensor_tensor(R["first"], R["rank"], bc(rc["best1"]), ALU.is_equal),
                    12: lambda: v.scalar_tensor_tensor(R["rest"], R["first"], -4.0, R["p"], ALU.mult, ALU.add),
                    13: lambda: v.tensor_reduce(rc["p2"][:, :], R["rest"], AX.X, ALU.max),
                    14: lambda: v.tensor_tensor(R["hit"], R["rest"], bc(rc["p2"]), ALU.is_equal),
                    15: lambda: v.tensor_tensor(R["rank"], R["hit"], priority[:, :, :], ALU.mult),
                    16: lambda: v.tensor_reduce(rc["best2"][:, :], R["rank"], AX.X, ALU.max),
                    17: lambda: v.tensor_tensor(R["second"], R["rank"], bc(rc["best2"]), ALU.is_equal),
                    18: lambda: v.tensor_tensor(rc["gap"][:, :], rc["p1"][:, :], rc["p2"][:, :], ALU.subtract),
                    19: lambda: v.tensor_tensor(R["both"], R["first"], R["second"], ALU.add),
                    20: lambda: v.tensor_tensor(R["diff"], R["first"], R["second"], ALU.subtract),
                    21: lambda: v.scalar_tensor_tensor(R["tilt"], R["diff"], 0.5, bc(rc["tanh"]), ALU.mult, ALU.mult),
                    22: lambda: v.scalar_tensor_tensor(R["w"], R["both"], 0.5, R["tilt"], ALU.mult, ALU.add),
                    23: lambda: v.tensor_copy(w_blocks[:, :, 0:4:2, 0:EXPERTS],
                                              R["w"].unsqueeze(2).to_broadcast([P, GB, 2, EXPERTS])),
                    24: lambda: v.tensor_tensor(w_blocks[:, :, 1:4:2, 0:EXPERTS],
                                                R["w"].unsqueeze(2).to_broadcast([P, GB, 2, EXPERTS]),
                                                w_blocks_f[:, :, 0:4:2, 0:EXPERTS], ALU.subtract),
                }
                for t in range(first, last + 1):
                    if t == 1:
                        dve.wait_ge(s_logits, c + 1)
                    if t == 4:
                        dve.wait_ge(s_route_act, 2 * c + 1)
                    if t == 21:
                        dve.wait_ge(s_route_act, 2 * c + 2)
                    if t == 23:
                        wait(dve, s_w_t, c)
                    if t not in (4, 19, 20):
                        wait(dve, s_route, ROUTE * c + t - 1)
                    steps[t]().then_inc(s_route, 1)

            def iteration(i, n, parity):
                static = isinstance(i, int)

                def route(d, first, last):
                    if live(i + d):
                        route_steps(n + d, first, last)

                def set_up(at, prepare):
                    if run == 0 and static and i == at:
                        prepare(dve)

                def statistics(norm, g, b):
                    done = v.bn_stats(stats[:, norm, b], X_of(g, b))
                    if b == GB - 1:
                        done.then_inc(s_stats[norm], 1)

                def statistics1(d, b):
                    if gnn and live(i + d):
                        if b == 0:
                            wait_apart(dve, s_rstd1, 3 * (n + d), s_ident)
                            dve.wait_ge(s_x_loaded[(parity + d) % 2], loads(i + d))
                        statistics(0, i + d, b)

                def statistics2(d, b):
                    if live(i + d):
                        if b == 0:
                            wait_apart(dve, s_rstd2, 3 * (n + d), s_ident)
                            if gnn:
                                dve.wait_ge(s_x1, n + d + 1)
                        statistics(1, i + d, b)

                def aggregate(norm, c):
                    wait_apart(dve, s_stats[norm], c + 1, s_ident)
                    for b in range(GB):
                        last = v.bn_aggr(mean_var[:, norm, b], stats[:, norm, b])
                    last.then_inc(s_mean_var[norm], 1)

                def aggregate1(d):
                    if gnn and live(i + d):
                        aggregate(0, n + d)

                def aggregate2(d):
                    if live(i + d):
                        aggregate(1, n + d)

                def add_eps(norm, c, s_ln):
                    dve.wait_ge(s_mean_var[norm], c + 1)
                    v.tensor_scalar(var_eps[:, norm], mean_var[:, norm, :, 1], LN_EPS, None, ALU.add)\
                        .then_inc(s_ln, 1)

                def add_eps1(d):
                    if gnn and live(i + d):
                        add_eps(0, n + d, s_ln1)

                def add_eps2(d):
                    if live(i + d):
                        add_eps(1, n + d, s_ln2)

                def normalise(norm, g, c, b, s_rstd, s_t, s_xn):
                    if b == 0:
                        dve.wait_ge(s_rstd, 3 * (c + 1))
                        wait(dve, s_t, c)
                    done = v.tensor_scalar(xn[:, norm, b * P:(b + 1) * P], X_of(g, b), centre[:, norm, b:b + 1],
                                           rstd[:, norm, b:b + 1], ALU.subtract, ALU.mult)
                    if b == GB - 1:
                        done.then_inc(s_xn, 1)

                def normalise1(d, b):
                    if gnn and live(i + d):
                        normalise(0, i + d, n + d, b, s_rstd1, s_t1, s_xn1)

                def normalise2(d, b):
                    if live(i + d):
                        normalise(1, i + d, n + d, b, s_rstd2, s_t2, s_xn2)

                def norm1_low(d):
                    if gnn and live(i + d):
                        dve.wait_ge(s_xg_hi, n + d + 1)
                        v.tensor_tensor(xg_lo[:, :], ps_b, xg_hi[:, :].bitcast(F32), ALU.subtract).then_inc(s_xg_lo, 1)

                def norm2_low(d):
                    if live(i + d):
                        buf = (parity + d) % 2
                        dve.wait_ge(s_xf_hi, n + d + 1)
                        v.tensor_tensor(xf_lo[:, buf], ps_a, xf_hi[:, buf].bitcast(F32), ALU.subtract)\
                            .then_inc(s_xf_lo, 1)

                def values(d):
                    if gnn and live(i + d):
                        dve.wait_ge(s_gate, n + d + 1)
                        wait(dve, s_vals_lo, n + d)
                        v.scalar_tensor_tensor(vals[:, :, :], gate[:, :, :], 1.0, ps_hg[:, :, 0:P], ALU.add, ALU.mult)\
                            .then_inc(s_vals, 1)

                def find_edges(d):
                    if gnn and live(i + d):
                        buf = (parity + d) % 2
                        dve.wait_ge(s_adj_loaded[buf], loads(i + d))
                        wait(dve, s_agg, n + d)
                        v.tensor_scalar(loop_edges[:, :], adj_in[:, buf], 1.0, None, ALU.is_equal)\
                            .then_inc(s_edges, 1)

                def collect_over(d):
                    if gnn and live(i + d):
                        buf = (parity + d) % 2
                        dve.wait_ge(s_over, n + d + 1)
                        wait(dve, s_over_all, n + d)
                        v.tensor_tensor(over_all[:, :], over_all[:, :], over_sum[:, buf:buf + 1], ALU.max)\
                            .then_inc(s_over_all, 1)

                def residual1(d):
                    if gnn and live(i + d):
                        dve.wait_ge(s_agg, n + d + 1)
                        v.scalar_tensor_tensor(X_of(i + d), ps_b, 0.0, X_of(i + d), ALU.max, ALU.add)\
                            .then_inc(s_x1, 1)

                def residual2(d):
                    if live(i + d):
                        dve.wait_ge(s_out_t, n + d + 1)
                        v.tensor_tensor(X_of(i + d), ps_a, X_of(i + d), ALU.add).then_inc(s_final, 1)

                def first_low(d, e):
                    if live(i + d):
                        k = EXPERTS * (n + d) + e
                        dve.wait_ge(s_r1_hi, k + 1)
                        v.scalar_tensor_tensor(r1_lo[:, e], ps_l1[e % 2][:, :], 0.0, r1_hi[:, e].bitcast(F32),
                                               ALU.max, ALU.subtract).then_inc(s_r1_lo, 1)

                def weigh(d, e):
                    if live(i + d):
                        k = EXPERTS * (n + d) + e
                        dve.wait_ge(s_u2, k + 1)
                        dve.wait_ge(s_wb, k + 1)
                        wait(dve, s_r2_lo, k - 1)
                        v.tensor_tensor(v2[:, e % 2], u2[:, e % 2], ps_w[:, :], ALU.mult).then_inc(s_v2, 1)

                weigh(-2, 4)
                route(-1, 16, 16)
                first_low(-1, 2)
                set_up(-2, prepare_hg)
                route(-1, 17, 17)
                norm2_low(0)
                route(-1, 18, 19)
                normalise1(2, 0)
                route(-1, 20, 20)
                weigh(-2, 5)
                normalise1(2, 1)
                route(-1, 21, 21)
                normalise1(2, 2)
                route(-1, 22, 22)
                normalise1(2, 3)
                route(-1, 23, 23)
                statistics1(3, 0)
                route(-1, 24, 24)
                set_up(-2, prepare_hg_parts)
                first_low(-1, 3)
                set_up(-1, prepare_first)
                residual1(1)
                first_low(-1, 4)
                statistics2(1, 0)
                statistics2(1, 1)
                statistics2(1, 2)
                weigh(-1, 0)
                route(0, 1, 1)
                statistics2(1, 3)
                route(0, 2, 2)
                collect_over(1)
                aggregate2(1)
                route(0, 3, 3)
                weigh(-1, 1)
                norm1_low(2)
                add_eps2(1)
                first_low(-1, 5)
                route(0, 4, 4)
                statistics1(3, 1)
                route(0, 5, 5)
                weigh(-1, 2)
                statistics1(3, 2)
                route(0, 6, 6)
                statistics1(3, 3)
                route(0, 7, 7)
                first_low(0, 0)
                route(0, 8, 8)
                residual2(-2)
                aggregate1(3)
                route(0, 9, 9)
                normalise2(1, 0)
                route(0, 10, 10)
                add_eps1(3)
                weigh(-1, 3)
                normalise2(1, 1)
                route(0, 11, 11)
                normalise2(1, 2)
                route(0, 12, 12)
                normalise2(1, 3)
                route(0, 13, 13)
                values(2)
                route(0, 14, 14)
                first_low(0, 1)
                route(0, 15, 15)
                find_edges(2)

            pipeline(dve, iteration, run)
            if gnn:
                dve.wait_ge(s_over_sum, 1)
                v.tensor_scalar(flag[:, :], ps_b[0:1, 0:1], 0.0, None, ALU.is_gt).then_inc(s_flag, 1)

        def pe_setup(pe):
            t = nc.tensor
            pe.wait_ge(s_hg_loaded, DMA * N_HG)
            pe.wait_ge(s_ident, 2)
            for n in range(2):
                t.transpose(ps_l1[0][:, n * P:(n + 1) * P], raw_loop[:, n], ident[:, :]).then_inc(s_loop_t, 1)
            pe.wait_ge(s_prep_hg, 1)
            t.matmul(ps_l1[1][:, 0:P], raw_loop[:, 0], wg_t[:, :], start=True, stop=True).then_inc(s_gate_w, 1)
            pe.wait_ge(s_const, 2)
            pe.wait_ge(s_prep_hg, 3)
            t.matmul(ps_l2[0][:, 0:2 * P], ones[:, :], hg[:, :, :].rearrange("p a b -> p (a b)"),
                     start=True, stop=True).then_inc(s_col_sums, 1)

        def pe_column_sums(pe):
            t = nc.tensor
            pe.wait_ge(s_w1_loaded, DMA * N_W1)
            t.matmul(ps_w[:, 0:P], ones[:, :], raw_router[:, :], start=True, stop=True).then_inc(s_col_sums, 1)
            pe.wait_ge(s_prep_hg, N_PREP_HG)
            half = EXPERTS // 2
            for n in range(2):
                last = t.matmul(ps_l2[n][:, 0:half * P], ones[:, :],
                                raw_w[0][:, n * half:(n + 1) * half].rearrange("p e f -> p (e f)"),
                                start=True, stop=True)
            last.then_inc(s_col_sums, 1)

        def pe_pipeline(pe, run):
            t = nc.tensor
            gnn = run == 0

            def product(ps, w_hi_, w_lo_, x_hi, x_lo, start=True):
                t.matmul(ps, w_hi_, x_hi, start=start, stop=False)
                t.matmul(ps, w_lo_, x_hi, start=False, stop=False)
                return t.matmul(ps, w_hi_, x_lo, start=False, stop=True)

            def transpose4(ps, tile):
                for b in range(GB):
                    last = t.transpose(ps[:, b * P:(b + 1) * P], tile[:, b * P:(b + 1) * P], ident[:, :])
                return last

            def iteration(i, n, parity):
                static = isinstance(i, int)

                def first_layer_parts(d):
                    if run == 0 and static and i + d == 0:
                        pe.wait_ge(s_prep, N_PREP)
                        pe.wait_ge(s_w1_lo, 1)

                def transpose_norm1(d):
                    if gnn and live(i + d):
                        pe.wait_ge(s_xn1, n + d + 1)
                        wait(pe, s_x1, n + d)
                        transpose4(ps_b, xn[:, 0]).then_inc(s_t1, 1)

                def set_up(at, prepare):
                    if run == 0 and static and i == at:
                        prepare(pe)

                def gate_products(d):
                    if gnn and live(i + d):
                        c = n + d
                        pe.wait_ge(s_xg_lo, c + 1)
                        if static and i + d == 0:
                            pe.wait_ge(s_prep_hg, N_PREP_HG)
                        if live(i + d - 4):
                            pe.wait_ge(s_final, c - 3)
                        elif live(i + d - 2):
                            pe.wait_ge(s_route, ROUTE * (c - 2) + 1)
                        hi, lo = (h[:, :, :].rearrange("p a b -> p (a b)") for h in (hg_hi, hg_lo))
                        for b in range(GB):
                            o = slice(b * P, (b + 1) * P)
                            ps = ps_side[:, b * 2 * P:(b + 1) * 2 * P]
                            t.matmul(ps, xg_hi[:, o], hi, start=True, stop=False)
                            t.matmul(ps, xg_hi[:, o], lo, start=False, stop=False)
                            last = t.matmul(ps, xg_lo[:, o], hi, start=False, stop=True)
                        last.then_inc(s_hg, 1)

                def sum_edges(d):
                    if gnn and live(i + d):
                        pe.wait_ge(s_edges, n + d + 1)
                        pe.wait_ge(s_vals_lo, n + d + 1)
                        for b in range(GB):
                            o = slice(b * P, (b + 1) * P)
                            t.matmul(ps_b[:, o], loop_edges[:, o], vals_hi[:, o], start=True, stop=False)
                            last = t.matmul(ps_b[:, o], loop_edges[:, o], vals_lo[:, o], start=False, stop=True)
                        last.then_inc(s_agg, 1)

                def transpose_norm2(d):
                    if live(i + d):
                        c = n + d
                        pe.wait_ge(s_xn2, c + 1)
                        if gnn and live(i + d + 1):
                            pe.wait_ge(s_vals, c + 2)
                        elif live(i + d - 3):
                            pe.wait_ge(s_final, c - 2)
                        elif live(i + d - 1):
                            pe.wait_ge(s_route, ROUTE * (c - 1) + 1)
                        transpose4(ps_a, xn[:, 1]).then_inc(s_t2, 1)

                def router_layer(d):
                    if live(i + d):
                        buf = (parity + d) % 2
                        first_layer_parts(d)
                        pe.wait_ge(s_xf_lo, n + d + 1)
                        product(ps_a, router_hi[:, :], router_lo[:, :], xf_hi[:, buf], xf_lo[:, buf]).then_inc(s_rh, 1)

                def logits(d):
                    if live(i + d):
                        if run == 0 and static and i + d == 0:
                            pe.wait_ge(s_rest_loaded, DMA * N_REST)
                        pe.wait_ge(s_router_h, n + d + 1)
                        for b in range(GB):
                            last = t.matmul(ps_a[:, b * EXPERTS:(b + 1) * EXPERTS], router_h[:, b * P:(b + 1) * P],
                                            logit_w[:, :], start=True, stop=True)
                        last.then_inc(s_logits, 1)

                def transpose_weights(d):
                    if live(i + d):
                        if run == 0 and static and i + d == 0:
                            pe.wait_ge(s_prep, N_PREP)
                        pe.wait_ge(s_route, ROUTE * (n + d + 1))
                        wait(pe, s_v2, EXPERTS * (n + d))
                        transpose4(ps_w, w_parts[:, :, :].rearrange("p b c -> p (b c)")).then_inc(s_w_t, 1)

                def spread_weight(d, e):
                    if live(i + d):
                        k = EXPERTS * (n + d) + e
                        if e == 0:
                            if run == 0 and static and i + d == 0:
                                pe.wait_ge(s_rest_lo, N_REST_LO)
                            pe.wait_ge(s_w_rows, n + d + 1)
                        wait(pe, s_v2, k)
                        t.matmul(ps_w[:, :], select[:, e], w_rows[:, :], start=True, stop=True).then_inc(s_wb, 1)

                def first_layer(d, e):
                    if live(i + d):
                        k = EXPERTS * (n + d) + e
                        buf = (parity + d) % 2
                        if e == 0:
                            first_layer_parts(d)
                            pe.wait_ge(s_xf_lo, n + d + 1)
                        wait(pe, s_r1_lo, k - 1)
                        product(ps_l1[e % 2][:, :], w_hi[0][:, e], w_lo[0][:, e], xf_hi[:, buf], xf_lo[:, buf])\
                            .then_inc(s_l1, 1)

                def second_layer(d, e):
                    if live(i + d):
                        k = EXPERTS * (n + d) + e
                        if run == 0 and static and k == 0:
                            pe.wait_ge(s_rest_lo, N_REST_LO)
                        pe.wait_ge(s_r1_lo, k + 1)
                        wait(pe, s_u2, k - 1)
                        product(ps_l2[e % 2][:, :], w_hi[1][:, e], w_lo[1][:, e], r1_hi[:, e], r1_lo[:, e])\
                            .then_inc(s_l2, 1)

                def third_layer(d, e):
                    if live(i + d):
                        k = EXPERTS * (n + d) + e
                        r = e % R2_RING
                        if e == 0:
                            wait(pe, s_ffn_t, n + d)
                            t.matmul(ps_l3[:, :], b3_split[:, :], w_rows[:, :], start=True, stop=False)
                        pe.wait_ge(s_r2_lo, k + 1)
                        t.matmul(ps_l3[:, :], w_hi[2][:, e], r2_hi[:, r], start=False, stop=False)
                        t.matmul(ps_l3[:, :], w_lo[2][:, e], r2_hi[:, r], start=False, stop=False)
                        t.matmul(ps_l3[:, :], w_hi[2][:, e], r2_lo[:, r], start=False, stop=e == EXPERTS - 1)\
                            .then_inc(s_l3, 1)

                def transpose_output(d):
                    if live(i + d):
                        c = n + d
                        pe.wait_ge(s_ffn_t, c + 1)
                        if live(i + d + 2):
                            pe.wait_ge(s_route, ROUTE * (c + 2) + 1)
                        else:
                            pe.wait_ge(s_final, c)
                        transpose4(ps_a, ffn_t).then_inc(s_out_t, 1)

                transpose_weights(-1)
                third_layer(-2, 4)
                logits(0)
                transpose_norm1(2)
                spread_weight(-1, 0)
                first_layer(-1, 5)
                second_layer(-1, 2)
                spread_weight(-1, 1)
                third_layer(-2, 5)
                second_layer(-1, 3)
                first_layer(0, 0)
                spread_weight(-1, 2)
                second_layer(-1, 4)
                transpose_output(-2)
                third_layer(-1, 0)
                first_layer(0, 1)
                spread_weight(-1, 3)
                second_layer(-1, 5)
                gate_products(2)
                first_layer(0, 2)
                second_layer(0, 0)
                spread_weight(-1, 4)
                third_layer(-1, 1)
                transpose_norm2(1)
                third_layer(-1, 2)
                first_layer(0, 3)
                spread_weight(-1, 5)
                second_layer(0, 1)
                first_layer(0, 4)
                set_up(-2, pe_column_sums)
                router_layer(1)
                sum_edges(2)
                third_layer(-1, 3)
                if gnn and static and i == GROUPS:
                    pe.wait_ge(s_over_all, GROUPS)
                    pe.wait_ge(s_x1, GROUPS)
                    t.matmul(ps_b[0:1, 0:1], over_all[:, :], ones[:, 0:1], start=True, stop=True)\
                        .then_inc(s_over_sum, 1)

            pipeline(pe, iteration, run)

        DIRECTIONS = [
            (w_fwd, wg_fwd, b_fwd, bg_fwd, RELS // REL_CHUNK, REL_CHUNK, True, 0),
            (w_bwd, wg_bwd, b_bwd, bg_bwd, RELS // REL_CHUNK, REL_CHUNK, False, RELS // REL_CHUNK * GRAPHS),
            (w_loop, wg_loop, b_loop, bg_loop, 1, 1, False, 2 * (RELS // REL_CHUNK) * GRAPHS),
        ]
        VISITS = (2 * (RELS // REL_CHUNK) + 1) * GRAPHS

        def visits(eng, direction, visit, per_chunk=None):
            chunks, before = DIRECTIONS[direction][4], DIRECTIONS[direction][7]
            with eng.Fori(0, chunks) as chunk:
                if per_chunk is not None:
                    per_chunk(chunk)
                with eng.Fori(0, GRAPHS) as graph:
                    visit(chunk, graph, chunk * GRAPHS + graph + before)

        def chunks_before(direction):
            return DIRECTIONS[direction][7] // GRAPHS

        def general_sp(sp):
            sp.wait_ge(s_final, GROUPS)
            sp.wait_ge(s_stored, DMA * GROUPS)
            for d, (w, wg, b, bg, chunks, rels, _, before) in enumerate(DIRECTIONS):
                wait(sp, s_gen_gate_w, d)
                sp.dma_start(raw_loop[:, 0], w).then_inc(s_gen_w_loaded, DMA)
                sp.dma_start(raw_loop[:, 1], wg).then_inc(s_gen_w_loaded, DMA)

                def per_chunk(chunk, b=b, bg=bg, rels=rels, before=before):
                    wait_apart(sp, s_gen_step, (chunk * GRAPHS + before) * GEN_STEPS + 1, s_ident)
                    for n, rows in enumerate((b, bg)):
                        sp.dma_start(gen_bias[:, n, 0:rels], rows[bass.ds(chunk * rels, rels), :].partition_broadcast(P))\
                            .then_inc(s_gen_bias, DMA)

                def visit(chunk, graph, v):
                    wait_apart(sp, s_gen_in, v * 2 + 1, s_ident)
                    sp.dma_start(gen_x[:, :], x[bass.ds(graph, 1)].rearrange("g p d -> p (g d)"))\
                        .then_inc(s_gen_loaded, DMA)
                    sp.dma_start(gen_adj[:, :], adj[bass.ds(graph, 1)].rearrange("g p n -> p (g n)"))\
                        .then_inc(s_gen_loaded, DMA)

                visits(sp, d, visit, per_chunk)
            sp.wait_ge(s_gen_acc, VISITS + 1)
            with sp.Fori(0, GRAPHS) as graph:
                wait_apart(sp, s_gen_x1, graph + 1, s_ident)
                sp.dma_start(gen_x[:, :], x[bass.ds(graph, 1)].rearrange("g p d -> p (g d)"))\
                    .then_inc(s_gen_x_loaded, DMA)

        def general_pool(pool):
            pool.wait_ge(s_final, GROUPS)
            for r in range(RELS + 1):
                nc.gpsimd.memset(gen_number[:, r:r + 1], float(r + 1)).then_inc(s_gen_const, 1)

            def visit(chunk, graph, v):
                pool.wait_ge(s_gen_var, v + 1)
                nc.gpsimd.tensor_tensor(rstd[:, 0, 0:1], var_eps[:, 0, 0:1], minus_half[:, 0:1], ALU.pow)\
                    .then_inc(s_gen_rstd, 1)

            for d in range(3):
                visits(pool, d, visit)

        def general_act(act):
            act.wait_ge(s_final, GROUPS)
            for d, (_, _, _, _, _, rels, _, _) in enumerate(DIRECTIONS):
                def visit(chunk, graph, v, rels=rels):
                    act.wait_ge(s_gen_step, v * GEN_STEPS + 3)
                    nc.scalar.activation(gen_gate[:, 0:rels], gen_gate[:, 0:rels], ACT.Tanh, scale=0.5)\
                        .then_inc(s_gen_gate, 1)

                visits(act, d, visit)

        def general_pe(pe):
            t = nc.tensor
            pe.wait_ge(s_final, GROUPS)
            pe.sem_inc(s_gen_sum, 1)
            for d, (_, _, _, _, _, rels, turned, _) in enumerate(DIRECTIONS):
                pe.wait_ge(s_gen_w_loaded, DMA * 2 * (d + 1))
                pe.wait_ge(s_gen_acc, DIRECTIONS[d][7] + 1)
                for n in range(2):
                    last = t.transpose(ps_l1[0][:, n * P:(n + 1) * P], raw_loop[:, n], ident[:, :])
                last.then_inc(s_gen_w_t, 1)
                pe.wait_ge(s_gen_w, 3 * d + 2)
                t.matmul(ps_l1[1][:, 0:P], raw_loop[:, 0], wg_t[:, :], start=True, stop=True)\
                    .then_inc(s_gen_gate_w, 1)
                pe.wait_ge(s_gen_w, 3 * d + 3)

                def visit(chunk, graph, v, rels=rels, turned=turned):
                    pe.wait_ge(s_gen_in, v * 2 + 3)
                    last = t.transpose(ps_l1[0][:, 0:P], gen_xn[:, :], ident[:, :])
                    if turned:
                        last = t.transpose(ps_l1[0][:, P:2 * P], gen_rel[:, :], ident[:, :])
                    last.then_inc(s_gen_t, 1)
                    pe.wait_ge(s_gen_t_copied, v * 2 + 2)
                    t.matmul(ps_l1[1][:, 0:2 * P], gen_xn_t[:, :], gen_w[:, :, :].rearrange("p a b -> p (a b)"),
                             start=True, stop=True).then_inc(s_gen_hg, 1)
                    pe.wait_ge(s_gen_step, (v + 1) * GEN_STEPS + 1)
                    pe.wait_ge(s_gen_acc, v + 1)
                    for r in range(rels):
                        last = t.matmul(ps_l2[0][:, 0:P], gen_hot[:, r], gen_vals[:, r], start=r == 0, stop=r == rels - 1)
                    last.then_inc(s_gen_sum, 1)

                visits(pe, d, visit)

        def general_dve(dve):
            v_ = nc.vector
            dve.wait_ge(s_final, GROUPS)
            dve.wait_ge(s_stored, DMA * GROUPS)
            for counter in (s_gen_in, s_gen_step, s_gen_acc, s_gen_x1):
                dve.sem_inc(counter, 1)
            v_.memset(X[:, :], 0.0).then_inc(s_gen_const, 1)
            dve.wait_ge(s_gen_const, RELS + 2)
            for d, (_, _, _, _, _, rels, turned, _) in enumerate(DIRECTIONS):
                dve.wait_ge(s_gen_w_t, d + 1)
                wait(dve, s_gen_hg, DIRECTIONS[d][7])
                v_.tensor_copy(gen_w[:, 0], ps_l1[0][:, 0:P]).then_inc(s_gen_w, 1)
                v_.tensor_copy(wg_t[:, :], ps_l1[0][:, P:2 * P]).then_inc(s_gen_w, 1)
                dve.wait_ge(s_gen_gate_w, d + 1)
                v_.tensor_copy(gen_w[:, 1], ps_l1[1][:, 0:P]).then_inc(s_gen_w, 1)
                big = [P, rels, P]

                def visit(chunk, graph, v, rels=rels, turned=turned, big=big, d=d):
                    node = X[:, bass.ds(graph * P, P)]
                    wait_apart(dve, s_gen_loaded, (v + 1) * 2 * DMA, s_ident)
                    v_.bn_stats(stats[:, 0, 0], gen_x[:, :]).then_inc(s_gen_stats, 1)
                    wait_apart(dve, s_gen_stats, v + 1, s_ident)
                    v_.bn_aggr(mean_var[:, 0, 0], stats[:, 0, 0]).then_inc(s_gen_mean, 1)
                    dve.wait_ge(s_gen_mean, v + 1)
                    v_.tensor_scalar(var_eps[:, 0, 0:1], mean_var[:, 0, 0, 1:2], LN_EPS, None, ALU.add)\
                        .then_inc(s_gen_var, 1)
                    dve.wait_ge(s_gen_rstd, v + 1)
                    v_.tensor_scalar(gen_xn[:, :], gen_x[:, :], mean_var[:, 0, 0, 0:1], rstd[:, 0, 0:1],
                                     ALU.subtract, ALU.mult).then_inc(s_gen_in, 1)
                    dve.wait_ge(s_gen_step, v * GEN_STEPS + 1)
                    v_.tensor_copy(gen_rel[:, :], gen_adj[:, :]).then_inc(s_gen_in, 1)
                    dve.wait_ge(s_gen_t, v + 1)
                    v_.tensor_copy(gen_xn_t[:, :], ps_l1[0][:, 0:P]).then_inc(s_gen_t_copied, 1)
                    rel = gen_rel_t if turned else gen_rel
                    if turned:
                        v_.tensor_copy(gen_rel_t[:, :], ps_l1[0][:, P:2 * P]).then_inc(s_gen_t_copied, 1)
                    else:
                        v_.tensor_copy(gen_rel_t[:, :], gen_rel[:, :]).then_inc(s_gen_t_copied, 1)
                    dve.wait_ge(s_gen_hg, v + 1)
                    v_.tensor_copy(gen_hg[:, :, :], ps_l1[1][:, 0:2 * P].rearrange("p (a b) -> p a b", a=2))\
                        .then_inc(s_gen_step, 1)
                    dve.wait_ge(s_gen_step, v * GEN_STEPS + 2)
                    dve.wait_ge(s_gen_bias, (chunk + chunks_before(d) + 1) * 2 * DMA)
                    v_.tensor_tensor(gen_gate[:, 0:rels], gen_bias[:, 1, 0:rels],
                                     gen_hg[:, 1].unsqueeze(1).to_broadcast(big), ALU.add).then_inc(s_gen_step, 1)
                    dve.wait_ge(s_gen_sum, v + 1)
                    v_.tensor_tensor(gen_vals[:, 0:rels], gen_bias[:, 0, 0:rels],
                                     gen_hg[:, 0].unsqueeze(1).to_broadcast(big), ALU.add).then_inc(s_gen_step, 1)
                    numbers = gen_number[:, 0:1] if d == 2 else gen_number[:, bass.ds(chunk * rels + 1, rels)]
                    dve.wait_ge(s_gen_t_copied, v * 2 + 2)
                    v_.tensor_tensor(gen_hot[:, 0:rels], rel[:, :].unsqueeze(1).to_broadcast(big),
                                     numbers.unsqueeze(2).to_broadcast(big), ALU.is_equal).then_inc(s_gen_step, 1)
                    dve.wait_ge(s_gen_gate, v + 1)
                    dve.wait_ge(s_gen_step, v * GEN_STEPS + 5)
                    v_.scalar_tensor_tensor(gen_vals[:, 0:rels], gen_gate[:, 0:rels], 1.0, gen_vals[:, 0:rels],
                                            ALU.add, ALU.mult).then_inc(s_gen_step, 1)
                    dve.wait_ge(s_gen_sum, v + 2)
                    dve.wait_ge(s_gen_acc, v + 1)
                    v_.scalar_tensor_tensor(node, ps_l2[0][:, 0:P], 0.5, node, ALU.mult, ALU.add)\
                        .then_inc(s_gen_acc, 1)

                visits(dve, d, visit)
            dve.wait_ge(s_gen_acc, VISITS + 1)
            with dve.Fori(0, GRAPHS) as graph:
                node = X[:, bass.ds(graph * P, P)]
                dve.wait_ge(s_gen_x_loaded, (graph + 1) * DMA)
                v_.scalar_tensor_tensor(node, node, 0.0, gen_x[:, :], ALU.max, ALU.add).then_inc(s_gen_x1, 1)
            dve.wait_ge(s_gen_x1, GRAPHS + 1)

        def if_general(eng, general, again):
            eng.wait_ge(s_flag, 1)
            found = eng.value_load(flag[0:1, 0:1], min_val=0, max_val=1)
            with eng.If_ne(eng.to_reg(found), 0):
                general(eng)
                again(eng, 1)

        with nc.Block() as block:
            @block.sync
            def _(sp):
                sp_pipeline(sp, 0)
                if_general(sp, general_sp, sp_pipeline)

            @block.gpsimd
            def _(pool):
                pool_constants(pool)
                pool_pipeline(pool, 0)
                if_general(pool, general_pool, pool_pipeline)

            @block.scalar
            def _(act):
                act_pipeline(act, 0)
                if_general(act, general_act, act_pipeline)

            @block.vector
            def _(dve):
                dve_pipeline(dve, 0)
                if_general(dve, general_dve, dve_pipeline)

            @block.tensor
            def _(pe):
                pe_setup(pe)
                pe_pipeline(pe, 0)
                if_general(pe, general_pe, pe_pipeline)


_INS = ['x', 'adj'] + ['L0_gnn_' + n for n in (
    'W_fwd', 'W_bwd', 'W_loop', 'Wg_fwd', 'Wg_bwd', 'Wg_loop', 'b_fwd', 'b_bwd', 'b_loop', 'bg_fwd', 'bg_bwd',
    'bg_loop')] + ['L0_ffn_' + n for n in (
        'router_w1', 'router_b1', 'router_w2', 'router_b2', 'expert_w1', 'expert_b1', 'expert_w2', 'expert_b2',
        'expert_w3', 'expert_b3')]


def kernel(**inputs):
    import numpy as _np
    import concourse.bacc as _bacc
    from concourse.bass_utils import run_bass_kernel_spmd as _run

    nc = _bacc.Bacc("TRN2", target_bir_lowering=False, num_devices=1)
    arrays, args = {}, []
    for name in _INS:
        a = _np.ascontiguousarray(inputs[name])
        arrays[f"in_{name}_dram"] = a
        args.append(nc.dram_tensor(f"in_{name}_dram", a.shape, mybir.dt.from_np(a.dtype), kind="ExternalInput").ap())
    out = nc.dram_tensor("out_0_dram", (GRAPHS, P, P), F32, kind="ExternalOutput").ap()
    adj_ffn_kernel(nc, *args, out)
    r = _run(nc, [arrays], core_ids=[0])
    return r.results[0]["out_0_dram"]
```
